# Optimizing a Trainium2 kernel written in Bass

```python
import numpy as np
import jax
import jax.numpy as jnp

def _softmax(x, axis=-1):
    return jax.nn.softmax(x, axis=axis)

def _gelu(x):
    return jax.nn.gelu(x, approximate=True)

def _silu(x):
    return jax.nn.silu(x)

def _sigmoid(x):
    return jax.nn.sigmoid(x)

def _layernorm(x, axis=-1, eps=1e-05):
    m = jnp.mean(x, axis=axis, keepdims=True)
    v = jnp.var(x, axis=axis, keepdims=True)
    return (x - m) / jnp.sqrt(v + eps)

def _scatter_add(tgt, idx, src, axis=0):
    return tgt.at[idx].add(src)

def _segment_sum(src, seg, n):
    return jax.ops.segment_sum(src, seg, n)
kernel_name = 'mk_xattn_ffn_d1_seqx_r4_7d979f'

def setup_inputs(seed: int=0):
    np.random.seed(seed)
    _w = jnp.asarray

    def _rec_inputs():
        import jax
        import jax.numpy as jnp
        _rk = jax.random.key(seed)
        x = -0.000125 + 0.9999 * jax.random.normal(jax.random.fold_in(_rk, 1), (2, 512, 1024), jnp.float32)
        _lenS = 512 - jax.random.randint(jax.random.fold_in(_rk, 7), (2,), 0, max(1, 512 // 4) + 1, jnp.int32)
        _lenS2 = 1024 - jax.random.randint(jax.random.fold_in(_rk, 8), (2,), 0, max(1, 1024 // 4) + 1, jnp.int32)
        _ctx_4096P = jax.random.normal(jax.random.fold_in(_rk, 11), (2, 16, 1024), jnp.float32)
        _ctx_4096c = jax.random.dirichlet(jax.random.fold_in(_rk, 511), 0.3 * jnp.ones((16,), jnp.float32), (2, 1024))
        _ctx_4096t = jnp.einsum('bsk,bkd->bsd', _ctx_4096c, _ctx_4096P)
        _ctx_4096t = _ctx_4096t * jax.lax.rsqrt(jnp.mean(jnp.square(_ctx_4096t)) + 1e-12) * 0.953939
        ctx_4096 = -5.72187e-05 + 0.999849 * (_ctx_4096t + 0.3 * jax.random.normal(jax.random.fold_in(_rk, 611), (2, 1024, 1024), jnp.float32))
        return (x, ctx_4096)
    x, ctx_4096 = _rec_inputs()

    def _L0_xattn_setup():
        import jax, jax.numpy as jnp
        import numpy as np
        QMIN = 0.0
        QMAX = 255.0

        def fake_quant(x, scale, zp):
            s = scale.reshape(())
            z = zp.reshape(())
            q = jnp.clip(jnp.round(x / s + z), QMIN, QMAX)
            return (q - z) * s
        key = jax.random.key(seed)
        k1, k2 = jax.random.split(key)
        B, M, K, N = (4, 512, 1024, 1024)
        x1 = jax.random.normal(k1, (B, M, K), dtype=jnp.float32)
        x2 = jax.random.normal(k2, (B, K, N), dtype=jnp.float32)
        x1_scale = jnp.full((1,), 8.0 / 255.0, dtype=jnp.float32)
        x1_zp = jnp.full((1,), 128.0, dtype=jnp.float32)
        x2_scale = jnp.full((1,), 8.0 / 255.0, dtype=jnp.float32)
        x2_zp = jnp.full((1,), 128.0, dtype=jnp.float32)
        return {'x1': x1, 'x2': x2, 'x1_scale': x1_scale, 'x1_zp': x1_zp, 'x2_scale': x2_scale, 'x2_zp': x2_zp}
    _L0_xattn_all = _L0_xattn_setup()
    _L0_xattn_in = {k: v for k, v in _L0_xattn_all.items() if k in ('x1_scale', 'x1_zp', 'x2_scale', 'x2_zp')}
    del _L0_xattn_all

    def _L0_ffn_setup():
        import jax, jax.numpy as jnp
        import numpy as np
        R = 16
        LORA_ALPHA = 16
        SCALING = LORA_ALPHA / R
        key = jax.random.key(seed)
        kx, kr, ka = jax.random.split(key, 3)
        B, S, D, DO, E = (4, 512, 1024, 1024, 8)
        x = jax.random.normal(kx, (B, S, D), dtype=jnp.float32)
        bound_r = 1.0 / np.sqrt(D)
        route_w = jax.random.uniform(kr, (E, D), jnp.float32, -bound_r, bound_r)
        bound_a = 1.0 / np.sqrt(D)
        A = jax.random.uniform(ka, (E, R, D), jnp.float32, -bound_a, bound_a)
        kb = jax.random.fold_in(key, 7)
        Bw = jax.random.normal(kb, (E, DO, R), dtype=jnp.float32) * 0.02
        return {'x': x, 'route_w': route_w, 'A': A, 'Bw': Bw}
    _L0_ffn_all = _L0_ffn_setup()
    _L0_ffn_in = {k: v for k, v in _L0_ffn_all.items() if k in ('route_w', 'A', 'Bw')}
    del _L0_ffn_all
    return {'x': x, 'ctx_4096': ctx_4096, 'L0_xattn_x1_scale': _L0_xattn_in['x1_scale'], 'L0_xattn_x1_zp': _L0_xattn_in['x1_zp'], 'L0_xattn_x2_scale': _L0_xattn_in['x2_scale'], 'L0_xattn_x2_zp': _L0_xattn_in['x2_zp'], 'L0_ffn_route_w': _L0_ffn_in['route_w'], 'L0_ffn_A': _L0_ffn_in['A'], 'L0_ffn_Bw': _L0_ffn_in['Bw']}

def reference(x, ctx_4096, L0_xattn_x1_scale, L0_xattn_x1_zp, L0_xattn_x2_scale, L0_xattn_x2_zp, L0_ffn_route_w, L0_ffn_A, L0_ffn_Bw):
    import jax
    import jax.numpy as jnp

    def _L0_xattn_ref(x1, x2, x1_scale, x1_zp, x2_scale, x2_zp):
        import jax, jax.numpy as jnp
        import numpy as np
        QMIN = 0.0
        QMAX = 255.0

        def fake_quant(x, scale, zp):
            s = scale.reshape(())
            z = zp.reshape(())
            q = jnp.clip(jnp.round(x / s + z), QMIN, QMAX)
            return (q - z) * s
        q1 = fake_quant(x1, x1_scale, x1_zp)
        q2 = fake_quant(x2, x2_scale, x2_zp)
        return jnp.matmul(q1, q2)

    def _L0_ffn_ref(x, route_w, A, Bw):
        import jax, jax.numpy as jnp
        import numpy as np
        R = 16
        LORA_ALPHA = 16
        SCALING = LORA_ALPHA / R
        logits = jnp.einsum('bsd,ed->bse', x, route_w)
        topk_v, topk_idx = jax.lax.top_k(logits, 1)
        E = logits.shape[-1]
        route_weight = jax.nn.one_hot(topk_idx[..., 0], E, dtype=logits.dtype) * topk_v
        h = jnp.einsum('bsd,erd->bser', x, A)
        wh = route_weight[..., None] * h
        out = jnp.einsum('bser,eor->bso', wh, Bw) * SCALING
        return out
    x = x + _L0_xattn_ref(_layernorm(x, axis=-1), ctx_4096, L0_xattn_x1_scale, L0_xattn_x1_zp, L0_xattn_x2_scale, L0_xattn_x2_zp)
    x = x + _L0_ffn_ref(_layernorm(x, axis=-1), L0_ffn_route_w, L0_ffn_A, L0_ffn_Bw)
    return x

_drawn_inputs = setup_inputs


def setup_inputs(seed=0):
    import zlib

    import numpy as np

    out = dict(_drawn_inputs(seed))
    spreads = {}
    factors = {'L0_ffn_route_w': 8.0, 'L0_ffn_A': 8.0, 'L0_ffn_Bw': 8.0}
    for name, (base, spread) in spreads.items():
        noise = np.random.default_rng([zlib.crc32(name.encode()), seed]).standard_normal(out[name].shape)
        drawn = base * np.exp(spread * noise) if base else spread * noise
        out[name] = jnp.asarray(drawn.astype(out[name].dtype))
    for name, factor in factors.items():
        out[name] = (out[name] * factor).astype(out[name].dtype)
    return out
```

```python
from contextlib import ExitStack

import concourse.bass as bass
from concourse import mybir

ALU = mybir.AluOpType
ACT = mybir.ActivationFunctionType
F32 = mybir.dt.float32
BF16 = mybir.dt.bfloat16
I16 = mybir.dt.int16
U8 = mybir.dt.uint8
U32 = mybir.dt.uint32
I32 = mybir.dt.int32

P = 128
EPS = 1e-5
QMAX = 255.0


def build(nc, x, ctx_in, s1, z1, s2, z2, route_w, lora_a, lora_b, out):
    B, S, D = x.shape
    N = ctx_in.shape[2]
    E, R, _ = lora_a.shape
    ER = E * R
    T = B * S // P
    TB = S // P
    K = D // P
    H = 512
    W = E + ER
    LAST = T - 1
    assert ER == P and N == 2 * H and D == N and TB == 4 and B == 2 and E == 8

    x_dram = x.rearrange("b s d -> (b s) d").rearrange("(t p) d -> t p d", p=P)
    out_dram = out.rearrange("b s d -> (b s) d").rearrange("(t p) d -> t p d", p=P)
    ctx_dram = ctx_in.rearrange("b (j c p) n -> b j p c n", p=P, c=2)
    a_dram = lora_a.rearrange("e r d -> (e r) d")
    b_dram = lora_b.rearrange("e (p c) r -> p e c r", p=P)

    with ExitStack() as stack:
        def sb(name, shape, dt):
            return stack.enter_context(nc.sbuf_tensor(name, shape, dt))

        def bank(name, shape, dt):
            return stack.enter_context(nc.psum_tensor(name, shape, dt))

        def sem(name):
            return stack.enter_context(nc.semaphore(name))

        x_all = sb("x_all", [P, T, D], F32)
        ctx_f = sb("ctx_f", [P, B, K, N], F32)
        ctx_r = sb("ctx_r", [P, 2, N], I16)
        ctx_r1 = sb("ctx_r1", [P, 2, 2, N], I16)
        q2 = sb("q2", [P, B * K, N], BF16)
        q1_u8 = sb("q1_u8", [P, 2, D], U8)
        a1 = sb("a1", [P, 2, D], BF16)
        a1T = sb("a1T", [P, 2, K, P], BF16)
        x2 = sb("x2", [P, 2, N], F32)
        x2T = sb("x2T", [P, 2, K, P], F32)
        a_nat = sb("a_nat", [P, D], F32)
        r_nat = sb("r_nat", [E, D], F32)
        b_nat = sb("b_nat", [P, E, K, R], F32)
        b_cols = sb("b_cols", [P, K, ER], F32)
        wT = sb("wT", [P, K, W], F32)
        bT = sb("bT", [P, N], F32)
        w_sum = sb("w_sum", [P, W], F32)
        lh = sb("lh", [P, W], F32)
        wh = sb("wh", [P, ER], F32)
        whT = sb("whT", [P, P], F32)
        ident = sb("ident", [P, P], F32)
        ident_b = sb("ident_b", [P, P], BF16)
        ones = sb("ones", [P, P], F32)
        expert = sb("expert", [P, ER], F32)
        stats1 = sb("stats1", [P, 12], F32)
        stats2 = sb("stats2", [P, 12], F32)
        mv1 = sb("mv1", [P, T, 2], F32)
        mv2 = sb("mv2", [P, 2], F32)
        ln1 = sb("ln1", [P, 5, 2], F32)
        root = sb("root", [P, 2], F32)
        scale1 = sb("scale1", [P, T], F32)
        shift1 = sb("shift1", [P, T], F32)
        a1_sum = sb("a1_sum", [P, T], F32)
        top8 = sb("top8", [P, 8], F32)
        top_at = sb("top_at", [P, 8], U32)
        small = sb("small", [P, 6], F32)
        u = sb("u", [P, 2], F32)
        given = sb("given", [P, 4], F32)
        zi_u8 = sb("zi_u8", [P, 1], U8)
        fixed = sb("fixed", [P, 12], F32)
        rest = sb("rest", [P, 3, P], BF16)
        rest_f = sb("rest_f", [P, 2, P], F32)
        flag = sb("flag", [P, 1], I32)
        g_s1, g_z1, g_s2, g_z2 = (given[:, i:i + 1] for i in range(4))
        r_s2, half_s1, zi1, neg_zi1, f1, k_f1, s12, neg_s12z2, tmp1, tmp2 = (fixed[:, i:i + 1] for i in range(10))

        p_t1 = bank("p_t1", [P, K * P], BF16)
        p_main = bank("p_main", [P, 2, H], F32)
        p_t2 = bank("p_t2", [P, 2, H], F32)
        p_s2 = bank("p_s2", [P, H], F32)
        p_s3 = bank("p_s3", [P, 2, H], F32)
        p_whT = p_s2[:, 256:256 + P]

        given_in = sem("given_in")
        x_in = [sem(f"x_in{i}") for i in range(2)]
        ctx_in_sem = [sem(f"ctx_in{j}") for j in range(K // 2)]
        a_in, r_in, b_in = sem("a_in"), sem("r_in"), sem("b_in")
        const_set, const_ready = sem("const_set"), sem("const_ready")
        fixed_ready = sem("fixed_ready")
        b_cols_ready = sem("b_cols_ready")
        dve_step = sem("dve_step")
        var1_ready, root_ready, ln1_ready = sem("var1_ready"), sem("root_ready"), sem("ln1_ready")
        q1_ready, a1_ready, t1_done, a1T_ready = sem("q1_ready"), sem("a1_ready"), sem("t1_done"), sem("a1T_ready")
        ctx_rounded = sem("ctx_rounded")
        q2_ready, q2_whole = sem("q2_ready"), sem("q2_whole")
        main_done, x2_ready, t2_done, x2T_ready = sem("main_done"), sem("x2_ready"), sem("t2_done"), sem("x2T_ready")
        s2_done, wh_ready, t3_done, whT_ready = sem("s2_done"), sem("wh_ready"), sem("t3_done"), sem("whT_ready")
        s3_done, res_ready = sem("s3_done"), sem("res_ready")
        out_stored = [sem(f"out_stored{i}") for i in range(2)]
        prep_done, wT_copied, bT_copied, w_sum_ready = sem("prep_done"), sem("wT_copied"), sem("bT_copied"), sem("w_sum_ready")

        block = stack.enter_context(nc.Block())

        @block.sync
        def _(sp):
            for i, s in enumerate((s1, z1, s2, z2)):
                sp.dma_start(given[:, i:i + 1], s.rearrange("(a b) -> a b", a=1).broadcast_to([P, 1])).then_inc(given_in, 16)
            for t in range(2):
                sp.dma_start(x_all[:, t, :], x_dram[t]).then_inc(x_in[t], 16)
            for j in range(K // 2):
                sp.dma_start(ctx_f[:, 0, 2 * j:2 * j + 2, :], ctx_dram[0, j]).then_inc(ctx_in_sem[j], 16)
            sp.dma_start(a_nat[:, :], a_dram).then_inc(a_in, 16)
            sp.dma_start(r_nat[:, :], route_w).then_inc(r_in, 16)
            sp.dma_start(b_nat[:, :, :, :], b_dram).then_inc(b_in, 16)
            with sp.Fori(1, T // 2) as i:
                for h in range(2):
                    sp.wait_ge(x_in[h], 16 * i)
                    sp.dma_start(x_all[:, bass.ds(2 * i + h, 1), :], x_dram[bass.ds(2 * i + h, 1)].rearrange("a p d -> p a d")).then_inc(x_in[h], 16)
            for j in range(K // 2):
                sp.wait_ge(ctx_in_sem[j], 16)
                sp.dma_start(ctx_f[:, 1, 2 * j:2 * j + 2, :], ctx_dram[1, j]).then_inc(ctx_in_sem[j], 16)
            with sp.Fori(0, T // 2) as i:
                for h in range(2):
                    sp.wait_ge(res_ready, 2 * i + h + 1)
                    sp.dma_start(out_dram[bass.ds(2 * i + h, 1)].rearrange("a p d -> p a d"), x_all[:, bass.ds(2 * i + h, 1), :]).then_inc(out_stored[h], 16)
            for h in range(2):
                sp.wait_ge(out_stored[h], 16 * (T // 2))

        @block.gpsimd
        def _(pool):
            nc.gpsimd.memset(ident[:, :], 0.0).then_inc(const_set, 1)
            nc.gpsimd.memset(ident_b[:, :], 0.0).then_inc(const_set, 1)
            nc.gpsimd.memset(ones[:, :], 1.0).then_inc(const_ready, 1)
            nc.gpsimd.iota(expert[:, :], [[1, E], [0, R]], base=0, channel_multiplier=0,
                           allow_small_or_imprecise_dtypes=True).then_inc(const_ready, 1)
            pool.wait_ge(const_set, 2)
            for m in (ident, ident_b):
                nc.gpsimd.affine_select(out=m[:, :], in_=m[:, :], compare_op=ALU.not_equal, fill=1.0, base=0,
                                        pattern=[[-1, P]], channel_multiplier=1).then_inc(const_ready, 1)
            pool.wait_ge(b_in, 16)
            nc.gpsimd.tensor_copy(b_cols[:, :, :].rearrange("p c (e r) -> p e c r", e=E), b_nat[:, :, :, :]).then_inc(b_cols_ready, 1)
            pool.wait_ge(fixed_ready, 1)
            for j in range(K // 2):
                pool.wait_ge(ctx_in_sem[j], 32)
                nc.gpsimd.tensor_scalar(ctx_r1[:, j % 2, :, :], ctx_f[:, 1, 2 * j:2 * j + 2, :], r_s2, g_z2,
                                        ALU.mult, ALU.add).then_inc(ctx_rounded, 1)
                pool.wait_ge(ctx_rounded, j + 1)
                nc.gpsimd.tensor_scalar(q2[:, K + 2 * j:K + 2 * j + 2, :], ctx_r1[:, j % 2, :, :], 0.0, QMAX,
                                        ALU.max, ALU.min).then_inc(q2_whole, 1)

        @block.scalar
        def _(act):
            def roots(j):
                act.wait_ge(var1_ready, j + 1)
                nc.scalar.activation(root[:, :], ln1[:, 0, :], ACT.Sqrt).then_inc(root_ready, 1)

            def quantise(t, p):
                nc.scalar.activation(q1_u8[:, p, :], x_all[:, bass.ds(t, 1), :].rearrange("p a d -> p (a d)"), ACT.Identity,
                                     scale=scale1[:, bass.ds(t, 1)], bias=shift1[:, bass.ds(t, 1)]).then_inc(q1_ready, 1)
                act.wait_ge(q1_ready, t + 1)
                nc.scalar.activation(a1[:, p, :], q1_u8[:, p, :], ACT.Identity, bias=neg_zi1,
                                     accum_out=a1_sum[:, bass.ds(t, 1)]).then_inc(a1_ready, 1)

            def copy_a1T(t, p):
                act.wait_ge(t1_done, t + 1)
                nc.scalar.copy(a1T[:, p, :, :].rearrange("p k m -> p (k m)"), p_t1[:, :]).then_inc(a1T_ready, 1)

            def copy_x2T(t, p):
                for h in range(2):
                    act.wait_ge(t2_done, 2 * t + h + 1)
                    nc.scalar.copy(x2T[:, p, 4 * h:4 * h + 4, :].rearrange("p k m -> p (k m)"), p_t2[:, h, :]).then_inc(x2T_ready, 1)

            roots(0)
            act.wait_ge(fixed_ready, 1)
            act.wait_ge(ln1_ready, 1)
            quantise(0, 0)
            quantise(1, 1)
            copy_a1T(0, 0)
            copy_a1T(1, 1)
            roots(1)
            for h in range(2):
                act.wait_ge(prep_done, h + 1)
                nc.scalar.copy(wT[:, 4 * h:4 * h + 4, E:W], p_t2[:, h, :].rearrange("p (k m) -> p k m", m=P)).then_inc(wT_copied, 1)
            act.wait_ge(prep_done, 3)
            nc.scalar.copy(wT[:, :, 0:E], p_s2[:, 0:K * E].rearrange("p (k e) -> p k e", e=E)).then_inc(wT_copied, 1)
            act.wait_ge(ln1_ready, 2)
            act.wait_ge(t1_done, 1)
            quantise(2, 0)
            roots(2)
            copy_x2T(0, 0)
            act.wait_ge(main_done, 2)
            copy_a1T(2, 0)
            act.wait_ge(t1_done, 2)
            quantise(3, 1)
            roots(3)
            with act.Fori(0, 2) as i:
                for p in range(2):
                    t = 2 * i + 2 + p
                    copy_x2T(t - 1, 1 - p)
                    act.wait_ge(main_done, 2 * t)
                    copy_a1T(t + 1, 1 - p)
                    if p == 0:
                        act.wait_ge(ln1_ready, i + 3)
                    act.wait_ge(t1_done, t + 1)
                    quantise(t + 2, p)
            copy_x2T(5, 1)
            act.wait_ge(main_done, 12)
            copy_a1T(7, 1)
            copy_x2T(6, 0)
            copy_x2T(7, 1)

        @block.vector
        def _(dve):
            class Steps:
                n = 0
                loop = 0

            LINKS = 2 * (3 + 5)

            def link(ins):
                Steps.n += 1
                ins.then_inc(dve_step, 1)
                dve.wait_ge(dve_step, Steps.loop + Steps.n)

            def tt(out, a, b, op):
                return nc.vector.tensor_tensor(out, a, b, op)

            dve.wait_ge(given_in, 64)
            nc.vector.reciprocal(r_s2, g_s2)
            nc.vector.tensor_copy(zi_u8[:, :], g_z1)
            nc.vector.tensor_scalar(half_s1, g_s1, 0.5, None, ALU.mult)
            link(tt(s12, g_s1, g_s2, ALU.mult))
            nc.vector.tensor_copy(zi1, zi_u8[:, :])
            link(nc.vector.scalar_tensor_tensor(out=neg_s12z2, in0=s12, scalar=-1.0, in1=g_z2, op0=ALU.mult, op1=ALU.mult))
            nc.vector.tensor_scalar(neg_zi1, zi1, -1.0, None, ALU.mult)
            link(tt(f1, g_z1, zi1, ALU.subtract))
            nc.vector.tensor_scalar(k_f1, f1, float(D), None, ALU.mult)
            dve.wait_ge(const_ready, 4)
            link(nc.vector.tensor_scalar(rest_f[:, 0, :], ones[:, :], f1, -1.0, ALU.mult, ALU.mult))
            link(nc.vector.tensor_copy(rest[:, 0, :], rest_f[:, 0, :]))
            link(tt(rest_f[:, 1, :], rest_f[:, 0, :], rest[:, 0, :], ALU.subtract))
            link(nc.vector.tensor_copy(rest[:, 1, :], rest_f[:, 1, :]))
            link(tt(rest_f[:, 0, :], rest_f[:, 1, :], rest[:, 1, :], ALU.subtract))
            nc.vector.tensor_copy(rest[:, 2, :], rest_f[:, 0, :]).then_inc(fixed_ready, 1)

            def ln1_stats(t):
                dve.wait_ge(x_in[t % 2], 16 * (t // 2 + 1))
                for h in range(2):
                    last = nc.vector.bn_stats(stats1[:, 6 * h:6 * h + 6], x_all[:, t, H * h:H * h + H])
                link(last)
                link(nc.vector.bn_aggr(mv1[:, t, :], stats1[:, :]))

            def ln1_root(j):
                nc.vector.tensor_scalar(ln1[:, 0, :], mv1[:, 2 * j:2 * j + 2, 1], EPS, None, ALU.add).then_inc(var1_ready, 1)

            def ln1_finish(j):
                pair = slice(2 * j, 2 * j + 2)
                dve.wait_ge(root_ready, j + 1)
                link(nc.vector.reciprocal(ln1[:, 1, :], root[:, :]))
                link(tt(ln1[:, 2, :], ln1[:, 0, :], ln1[:, 1, :], ALU.mult))
                link(tt(ln1[:, 3, :], ln1[:, 2, :], root[:, :], ALU.add))
                link(nc.vector.tensor_scalar(ln1[:, 4, :], ln1[:, 3, :], half_s1, None, ALU.mult))
                link(nc.vector.reciprocal(scale1[:, pair], ln1[:, 4, :]))
                link(tt(ln1[:, 1, :], mv1[:, pair, 0], scale1[:, pair], ALU.mult))
                nc.vector.tensor_scalar(shift1[:, pair], ln1[:, 1, :], -1.0, g_z1, ALU.mult, ALU.add).then_inc(ln1_ready, 1)

            ln1_stats(0)
            ln1_stats(1)
            ln1_root(0)
            ln1_finish(0)
            for k in range(K):
                if k % 2 == 0:
                    dve.wait_ge(ctx_in_sem[k // 2], 16)
                link(nc.vector.tensor_scalar(ctx_r[:, k % 2, :], ctx_f[:, 0, k, :], r_s2, g_z2, ALU.mult, ALU.add))
                nc.vector.tensor_scalar(q2[:, k, :], ctx_r[:, k % 2, :], 0.0, QMAX, ALU.max, ALU.min).then_inc(q2_ready, 1)

            dve.wait_ge(q2_ready, K)
            nc.vector.tensor_scalar(flag[:, :], f1, 0.0, None, ALU.not_equal).then_inc(q2_whole, 1)

            def join_main(t, p, h):
                dve.wait_ge(main_done, 2 * t + h + 1)
                nc.vector.scalar_tensor_tensor(
                    out=x2[:, p, H * h:H * h + H], in0=p_main[:, h, :], scalar=s12,
                    in1=x_all[:, bass.ds(t, 1), H * h:H * h + H].rearrange("p a d -> p (a d)"), op0=ALU.mult, op1=ALU.add).then_inc(x2_ready, 1)

            def ln2_stats(t, p):
                dve.wait_ge(x2_ready, 2 * t + 2)
                for h in range(2):
                    last = nc.vector.bn_stats(stats2[:, 6 * h:6 * h + 6], x2[:, p, H * h:H * h + H])
                link(last)
                nc.vector.tensor_scalar(u[:, p:p + 1], a1_sum[:, bass.ds(t, 1)], k_f1, neg_s12z2, ALU.subtract, ALU.mult)
                link(nc.vector.bn_aggr(mv2[:, :], stats2[:, :]))
                nc.vector.tensor_scalar(small[:, 0:1], mv2[:, 0:1], -1.0, None, ALU.mult)
                link(nc.vector.tensor_scalar(small[:, 1:2], mv2[:, 1:2], EPS, None, ALU.add))

            def route(t):
                dve.wait_ge(s2_done, t + 1)
                link(nc.vector.scalar_tensor_tensor(out=lh[:, :], in0=w_sum[:, :], scalar=small[:, 0:1], in1=p_s2[:, 0:W],
                                                    op0=ALU.mult, op1=ALU.add))
                nc.vector.reciprocal(small[:, 2:3], small[:, 1:2])
                link(nc.vector.max(top8[:, :], lh[:, 0:E]))
                nc.vector.tensor_scalar(small[:, 3:4], top8[:, 0:1], small[:, 2:3], None, ALU.mult)
                link(nc.vector.max_index(top_at[:, :], top8[:, :], lh[:, 0:E]))
                link(nc.vector.tensor_copy(small[:, 4:5], top_at[:, 0:1]))
                link(nc.vector.scalar_tensor_tensor(out=wh[:, :], in0=expert[:, :], scalar=small[:, 4:5], in1=lh[:, E:W],
                                                    op0=ALU.is_equal, op1=ALU.mult))
                nc.vector.tensor_scalar(wh[:, :], wh[:, :], small[:, 3:4], None, ALU.mult).then_inc(wh_ready, 1)

            def copy_whT(t):
                dve.wait_ge(t3_done, t + 1)
                nc.vector.tensor_copy(whT[:, :], p_whT).then_inc(whT_ready, 1)

            def finish(t, p):
                for h in range(2):
                    dve.wait_ge(s3_done, 2 * t + h + 1)
                    last = nc.vector.scalar_tensor_tensor(out=x_all[:, bass.ds(t, 1), H * h:H * h + H].rearrange("p a d -> p (a d)"), in0=p_s3[:, h, :], scalar=u[:, p:p + 1],
                                                          in1=x2[:, p, H * h:H * h + H], op0=ALU.add, op1=ALU.add)
                last.then_inc(res_ready, 1)

            for t in range(2, 6):
                ln1_stats(t)
            ln1_root(1)
            ln1_finish(1)
            ln1_root(2)
            for h in range(2):
                dve.wait_ge(prep_done, 4 + h)
                nc.vector.tensor_copy(bT[:, :].rearrange("q (p c) -> q c p", c=K)[:, 4 * h:4 * h + 4, :],
                                      p_s3[:, h, :].rearrange("q (c p) -> q c p", p=P)).then_inc(bT_copied, 1)
            dve.wait_ge(prep_done, 6)
            nc.vector.tensor_copy(w_sum[:, :], p_s2[:, 0:W]).then_inc(w_sum_ready, 1)
            join_main(0, 0, 0)
            join_main(0, 0, 1)
            ln2_stats(0, 0)
            ln1_finish(2)
            for t in range(6, 8):
                ln1_stats(t)
            ln1_root(3)
            ln1_finish(3)
            join_main(1, 1, 0)
            dve.wait_ge(w_sum_ready, 1)
            route(0)
            before = Steps.n
            with dve.Fori(0, 3) as i:
                Steps.loop = i * LINKS
                for p in range(2):
                    t = 2 * i + 2 + p
                    join_main(t - 1, 1 - p, 1)
                    copy_whT(t - 2)
                    ln2_stats(t - 1, 1 - p)
                    finish(t - 2, p)
                    dve.wait_ge(res_ready, t - 1)
                    join_main(t, p, 0)
                    route(t - 1)
            assert Steps.n - before == LINKS
            Steps.n, Steps.loop = before + 3 * LINKS, 0
            join_main(7, 1, 1)
            copy_whT(6)
            ln2_stats(7, 1)
            finish(6, 0)
            route(7)
            copy_whT(7)
            finish(7, 1)

        @block.tensor
        def _(pe):
            def transpose_a1(t, p):
                pe.wait_ge(a1_ready, t + 1)
                pe.wait_ge(a1T_ready, t)
                for k in range(K):
                    last = nc.tensor.transpose(p_t1[:, P * k:P * k + P], a1[:, p, P * k:P * k + P], ident_b[:, :])
                last.then_inc(t1_done, 1)

            def main(b, p, h, k0, k1, arrivals=False):
                for k in range(k0, k1):
                    if arrivals:
                        pe.wait_ge(q2_ready, k + 1)
                    last = nc.tensor.matmul(p_main[:, h, :], a1T[:, p, k, :], q2[:, bass.ds(b * K + k, 1), H * h:H * h + H].rearrange("p a n -> p (a n)"),
                                            start=(k == 0), stop=(k == K - 1))
                if k1 == K:
                    last.then_inc(main_done, 1)

            def transpose_x2(t, p):
                pe.wait_ge(x2_ready, 2 * t + 2)
                pe.wait_ge(x2T_ready, 2 * t)
                for h in range(2):
                    for k in range(4 * h, 4 * h + 4):
                        last = nc.tensor.transpose(p_t2[:, h, P * (k % 4):P * (k % 4) + P], x2[:, p, P * k:P * k + P], ident[:, :])
                    last.then_inc(t2_done, 1)

            def logits_and_h(t, p):
                pe.wait_ge(whT_ready, t)
                for k in range(K):
                    if k % 4 == 0:
                        pe.wait_ge(x2T_ready, 2 * t + k // 4 + 1)
                    last = nc.tensor.matmul(p_s2[:, 0:W], x2T[:, p, k, :], wT[:, k, :], start=(k == 0), stop=(k == K - 1))
                last.then_inc(s2_done, 1)

            def transpose_wh(t):
                pe.wait_ge(wh_ready, t + 1)
                nc.tensor.transpose(p_whT, wh[:, :], ident[:, :]).then_inc(t3_done, 1)

            def lora_out(t):
                pe.wait_ge(whT_ready, t + 1)
                for h in range(2):
                    nc.tensor.matmul(p_s3[:, h, :], whT[:, :], bT[:, H * h:H * h + H], start=True, stop=True).then_inc(s3_done, 1)

            def period(t, p, b, more=True):
                pe.wait_ge(a1T_ready, t + 1)
                pe.wait_ge(x2_ready, 2 * t - 1)
                main(b, p, 0, 0, 4)
                lora_out(t - 2)
                transpose_x2(t - 1, 1 - p)
                main(b, p, 0, 4, K)
                if more:
                    transpose_a1(t + 1, 1 - p)
                logits_and_h(t - 1, 1 - p)
                main(b, p, 1, 0, K)
                transpose_wh(t - 1)

            pe.wait_ge(const_ready, 4)
            transpose_a1(0, 0)
            pe.wait_ge(a1T_ready, 1)
            main(0, 0, 0, 0, K, arrivals=True)
            transpose_a1(1, 1)
            pe.wait_ge(a_in, 16)
            for h in range(2):
                for k in range(4 * h, 4 * h + 4):
                    last = nc.tensor.transpose(p_t2[:, h, P * (k % 4):P * (k % 4) + P], a_nat[:, P * k:P * k + P], ident[:, :])
                last.then_inc(prep_done, 1)
            pe.wait_ge(r_in, 16)
            for k in range(K):
                last = nc.tensor.transpose(p_s2[:, E * k:E * k + E], r_nat[:, P * k:P * k + P], ident[0:E, 0:E])
            last.then_inc(prep_done, 1)
            pe.wait_ge(b_cols_ready, 1)
            for h in range(2):
                for c in range(4 * h, 4 * h + 4):
                    last = nc.tensor.transpose(p_s3[:, h, P * (c % 4):P * (c % 4) + P], b_cols[:, c, :], ident[:, :])
                last.then_inc(prep_done, 1)
            main(0, 0, 1, 0, K)
            pe.wait_ge(wT_copied, 3)
            for k in range(K):
                last = nc.tensor.matmul(p_s2[:, 0:W], ones[:, :], wT[:, k, :], start=(k == 0), stop=(k == K - 1))
            last.then_inc(prep_done, 1)
            pe.wait_ge(a1T_ready, 2)
            pe.wait_ge(x2_ready, 1)
            main(0, 1, 0, 0, 4)
            transpose_x2(0, 0)
            main(0, 1, 0, 4, K)
            transpose_a1(2, 0)
            pe.wait_ge(w_sum_ready, 1)
            pe.wait_ge(bT_copied, 2)
            logits_and_h(0, 0)
            main(0, 1, 1, 0, K)
            transpose_wh(0)
            with pe.Fori(0, 2) as i:
                pe.wait_ge(q2_whole, 4 * i + 1)
                for p in range(2):
                    period(2 * i + 2 + p, p, i)
            period(6, 0, 1)
            period(7, 1, 1, more=False)
            pe.wait_ge(res_ready, 6)
            lora_out(6)
            transpose_x2(7, 1)
            logits_and_h(7, 1)
            transpose_wh(7)
            pe.wait_ge(res_ready, 7)
            lora_out(7)


_INS = ['x', 'ctx_4096', 'L0_xattn_x1_scale', 'L0_xattn_x1_zp', 'L0_xattn_x2_scale', 'L0_xattn_x2_zp',
        'L0_ffn_route_w', 'L0_ffn_A', 'L0_ffn_Bw']
_OUTS = [((2, 512, 1024), 'float32')]


def kernel(**inputs):
    import numpy as _np
    import concourse.bacc as _bacc
    from concourse import mybir as _mybir
    from concourse.bass_utils import run_bass_kernel_spmd as _run

    nc = _bacc.Bacc("TRN2", target_bir_lowering=False, num_devices=1)
    arrays, args = {}, []
    for name in _INS:
        a = _np.ascontiguousarray(inputs[name])
        arrays[f"in_{name}_dram"] = a
        args.append(nc.dram_tensor(f"in_{name}_dram", a.shape, _mybir.dt.from_np(a.dtype), kind="ExternalInput").ap())
    for i, (shape, dtype) in enumerate(_OUTS):
        dt = _mybir.dt.from_np(_np.dtype(dtype))
        args.append(nc.dram_tensor(f"out_{i}_dram", shape, dt, kind="ExternalOutput").ap())
    build(nc, *args)
    r = _run(nc, [arrays], core_ids=[0])
    got = tuple(r.results[0][f"out_{i}_dram"] for i in range(len(_OUTS)))
    return got[0]
```

```python
from contextlib import ExitStack

import concourse.bass as bass
from concourse import mybir

ALU = mybir.AluOpType
ACT = mybir.ActivationFunctionType
F32 = mybir.dt.float32
BF16 = mybir.dt.bfloat16
I16 = mybir.dt.int16
F32R = mybir.dt.float32r
U8 = mybir.dt.uint8
U32 = mybir.dt.uint32
I32 = mybir.dt.int32

P = 128
EPS = 1e-5
QMAX = 255.0


def build(nc, x, ctx_in, given_in, w_in, b_in, out):
    B, S, D = x.shape
    N = ctx_in.shape[2]
    ER = b_in.shape[0]
    T = B * S // P
    K = D // P
    H = 512
    W = w_in.shape[1] // K
    E = W - ER
    R = ER // E
    assert ER == P and N == 2 * H and D == N and T == 8 and K == 8 and B == 2 and E == 8

    x_dram = x.rearrange("b s d -> (b s) d").rearrange("(t p) d -> t p d", p=P)
    out_dram = out.rearrange("b s d -> (b s) d").rearrange("(t p) d -> t p d", p=P)
    ctx_dram = ctx_in.rearrange("b (j c p) n -> b j p c n", p=P, c=2)

    with ExitStack() as stack:
        def sb(name, shape, dt):
            return stack.enter_context(nc.sbuf_tensor(name, shape, dt))

        def bank(name, shape, dt):
            return stack.enter_context(nc.psum_tensor(name, shape, dt))

        def sem(name):
            return stack.enter_context(nc.semaphore(name))

        x_all = sb("x_all", [P, T, D], F32)
        ctx_f = sb("ctx_f", [P, B, K, N], F32)
        ctx_r = sb("ctx_r", [P, 2, N], I16)
        ctx_rp = sb("ctx_rp", [P, 4, N], I16)
        q2 = sb("q2", [P, B * K, N], BF16)
        q1_u8 = sb("q1_u8", [P, 2, D], U8)
        a1 = sb("a1", [P, 2, D], BF16)
        a1T = sb("a1T", [P, 2, K, P], BF16)
        x2 = sb("x2", [P, 3, N], F32)
        x2T = sb("x2T", [P, 2, K, P], F32)
        squares = sb("squares", [P, N], BF16)
        wT = sb("wT", [P, K, W], F32)
        bT = sb("bT", [P, N], F32)
        b_hi = sb("b_hi", [P, N], F32R)
        b_lo = sb("b_lo", [P, N], F32R)
        w_fold = sb("w_fold", [P, 7, W], F32)
        w_sum = sb("w_sum", [P, W], F32)
        lh = sb("lh", [P, 2, W], F32)
        wh = sb("wh", [P, ER], F32)
        whT_hi = sb("whT_hi", [P, P], F32R)
        whT_lo = sb("whT_lo", [P, P], F32R)
        ident = sb("ident", [P, P], F32)
        ident_b = sb("ident_b", [P, P], BF16)
        ones = sb("ones", [P, P], F32)
        expert = sb("expert", [P, ER], F32)
        stats = sb("stats", [P, 12], F32)
        mean_var = sb("mean_var", [P, 2], F32)
        ln1 = sb("ln1", [P, 8, T], F32)
        scale1 = sb("scale1", [P, T], F32)
        shift1 = sb("shift1", [P, T], F32)
        a1_sum = sb("a1_sum", [P, T], F32)
        ln2 = sb("ln2", [P, 8, T], F32)
        top8 = sb("top8", [P, 8], F32)
        top_at = sb("top_at", [P, 8], U32)
        given = sb("given", [P, 4], F32)
        zi_u8 = sb("zi_u8", [P, 1], U8)
        fixed = sb("fixed", [P, 9], F32)
        rest = sb("rest", [P, 3, P], BF16)
        rest_f = sb("rest_f", [P, 2, P], F32)
        flag = sb("flag", [P, 1], I32)
        g_s1, g_z1, g_s2, g_z2 = (given[:, i:i + 1] for i in range(4))
        r_s1, r_s2, zi1, neg_zi1, f1, k_f1, s12, neg_s12z2, neg_s12 = (fixed[:, i:i + 1] for i in range(9))
        MEAN, VAR, INV, ROOT, E1, E2, E3, NSCALE = range(8)
        SUM0, SUM1, NMEAN, SQSUM, VAR2, INV2, COEF, U = range(8)

        p_t1 = bank("p_t1", [P, K * P], BF16)
        p_main = bank("p_main", [P, 2, H], F32)
        p_t2 = bank("p_t2", [P, 2, H], F32)
        p_s2 = bank("p_s2", [P, H], F32)
        p_s3 = bank("p_s3", [P, 2, H], F32)
        p_whT = p_s2[:, 256:256 + P]

        given_landed = sem("given_landed")
        x0_half = sem("x0_half")
        x_in = [sem(f"x_in{i}") for i in range(2)]
        ctx_sem = [sem(f"ctx_in{j}") for j in range(K // 2)]
        w_landed, b_landed = sem("w_landed"), sem("b_landed")
        const_set, const_ready = sem("const_set"), sem("const_ready")
        fixed_ready, rest_ready = sem("fixed_ready"), sem("rest_ready")
        dve_step, pool_step = sem("dve_step"), sem("pool_step")
        inv1_ready, root_ready, ln1_ready = sem("inv1_ready"), sem("root_ready"), sem("ln1_ready")
        q1_ready, a1_ready, t1_done, a1T_ready = sem("q1_ready"), sem("a1_ready"), sem("t1_done"), sem("a1T_ready")
        pool_rounded, q2_ready = sem("pool_rounded"), sem("q2_ready")
        pool_clipped = sem("pool_clipped")
        main_done, x2_ready, t2_done, x2T_ready = sem("main_done"), sem("x2_ready"), sem("t2_done"), sem("x2T_ready")
        mean2_ready, sq_ready = sem("mean2_ready"), sem("sq_ready")
        s2_done, wh_ready, t3_done = sem("s2_done"), sem("wh_ready"), sem("t3_done")
        whT_hi_ready, whT_ready = sem("whT_hi_ready"), sem("whT_ready")
        s3_done, res_ready = sem("s3_done"), sem("res_ready")
        out_stored = [sem(f"out_stored{i}") for i in range(2)]
        last_stored = [sem(f"last_stored{i}") for i in range(4)]
        w_folded = sem("w_folded")
        w_sum_done, w_sum_ready, b_hi_ready, b_lo_ready = sem("w_sum_done"), sem("w_sum_ready"), sem("b_hi_ready"), sem("b_lo_ready")

        block = stack.enter_context(nc.Block())
        POOL_ROUNDS = ((0, 3), (0, 5)) + tuple((1, k) for k in range(K))

        READ_AT = (4, 6) + tuple(K + k + 1 for k in range(K))

        @block.sync
        def _(sp):
            def load_x(t):
                if t >= 2:
                    sp.wait_ge(x_in[t % 2], 16 * (t // 2))
                sp.dma_start(x_all[:, t, :], x_dram[t]).then_inc(x_in[t % 2], 16)

            def load_ctx(b, j):
                if b:
                    sp.wait_ge(ctx_sem[j], 16)
                sp.dma_start(ctx_f[:, b, 2 * j:2 * j + 2, :], ctx_dram[b, j]).then_inc(ctx_sem[j], 16)

            sp.dma_start(x_all[:, 0, 0:H], x_dram[0][:, 0:H]).then_inc(x0_half, 16)
            sp.dma_start(x_all[:, 0, H:D], x_dram[0][:, H:D]).then_inc(x_in[0], 16)
            load_x(1)
            for j in range(3):
                load_ctx(0, j)
            load_x(2)
            load_ctx(0, 3)
            sp.dma_start(wT[:, :, :], w_in.rearrange("p (k w) -> p k w", w=W)).then_inc(w_landed, 16)
            load_x(3)
            sp.dma_start(bT[:, :], b_in).then_inc(b_landed, 16)
            load_x(4)
            for j in range(3):
                load_ctx(1, j)
            load_x(5)
            load_ctx(1, 3)
            load_x(6)
            load_x(7)
            with sp.Fori(0, T // 2 - 1) as i:
                for j in range(2):
                    sp.wait_ge(res_ready, 4 * i + 2 * j + 2)
                    sp.dma_start(out_dram[bass.ds(2 * i + j, 1)].rearrange("a p d -> p a d"), x_all[:, bass.ds(2 * i + j, 1), :]).then_inc(out_stored[j], 16)
            for t in range(T - 2, T):
                for h in range(2):
                    sp.wait_ge(res_ready, 2 * t + h + 1)
                    sp.dma_start(out_dram[t][:, H * h:H * h + H], x_all[:, t, H * h:H * h + H]).then_inc(last_stored[2 * (t % 2) + h], 16)
            for h in range(2):
                sp.wait_ge(out_stored[h], 16 * (T // 2 - 1))
            for stored in last_stored:
                sp.wait_ge(stored, 16)

        @block.gpsimd
        def _(pool):
            steps = [0]

            def link(ins):
                steps[0] += 1
                ins.then_inc(pool_step, 1)
                pool.wait_ge(pool_step, steps[0])

            nc.gpsimd.memset(ident_b[:, :], 0.0).then_inc(const_set, 1)
            nc.gpsimd.memset(ident[:, :], 0.0).then_inc(const_set, 1)
            for n, m in enumerate((ident_b, ident)):
                pool.wait_ge(const_set, n + 1)
                nc.gpsimd.affine_select(out=m[:, :], in_=m[:, :], compare_op=ALU.not_equal, fill=1.0, base=0,
                                        pattern=[[-1, P]], channel_multiplier=1).then_inc(const_ready, 1)
            nc.gpsimd.memset(ones[:, :], 1.0).then_inc(const_ready, 1)
            nc.gpsimd.iota(expert[:, :], [[1, E], [0, R]], base=0, channel_multiplier=0,
                           allow_small_or_imprecise_dtypes=True).then_inc(const_ready, 1)

            def ln1_finish(t):
                def col(i):
                    return ln1[:, i, t:t + 1]
                pool.wait_ge(root_ready, t + 1)
                link(nc.gpsimd.tensor_tensor(col(E1), col(ROOT), col(ROOT), ALU.mult))
                link(nc.gpsimd.tensor_tensor(col(E2), col(E1), col(VAR), ALU.mult))
                link(nc.gpsimd.tensor_scalar(col(E3), col(E2), 0.5, -1.5, ALU.mult, ALU.add))
                link(nc.gpsimd.tensor_scalar(col(NSCALE), col(E3), col(ROOT), r_s1, ALU.mult, ALU.mult))
                nc.gpsimd.tensor_scalar(scale1[:, t:t + 1], col(NSCALE), -1.0, 1.0, ALU.mult, ALU.mult)
                nc.gpsimd.tensor_scalar(shift1[:, t:t + 1], col(NSCALE), col(MEAN), g_z1,
                                        ALU.mult, ALU.add).then_inc(ln1_ready, 1)

            def round_ctx(n):
                b, k = POOL_ROUNDS[n]
                pool.wait_ge(ctx_sem[k // 2], 16 * (b + 1))
                if n >= 4:
                    pool.wait_ge(q2_ready, READ_AT[n - 4])
                nc.gpsimd.tensor_scalar(ctx_rp[:, n % 4, :], ctx_f[:, b, k, :], r_s2, g_z2, ALU.mult, ALU.add).then_inc(pool_rounded, 1)

            pool.wait_ge(fixed_ready, 1)
            pool.wait_ge(ln1_ready, 1)
            ln1_finish(1)
            round_ctx(0)
            round_ctx(1)
            ln1_finish(2)
            pool.wait_ge(w_landed, 16)
            link(nc.gpsimd.tensor_tensor(w_fold[:, 0:4, :], wT[:, 0:4, :], wT[:, 4:8, :], ALU.add))
            link(nc.gpsimd.tensor_tensor(w_fold[:, 4:6, :], w_fold[:, 0:2, :], w_fold[:, 2:4, :], ALU.add))
            nc.gpsimd.tensor_tensor(w_fold[:, 6, :], w_fold[:, 4, :], w_fold[:, 5, :], ALU.add).then_inc(w_folded, 1)
            ln1_finish(3)
            for n in range(2, 2 + K):
                round_ctx(n)
                if n == 3:
                    ln1_finish(4)
            ln1_finish(5)
            ln1_finish(6)
            ln1_finish(7)

        @block.scalar
        def _(act):
            def ln1_root(t):
                act.wait_ge(inv1_ready, t + 1)
                nc.scalar.activation(ln1[:, ROOT, bass.ds(t, 1)], ln1[:, INV, bass.ds(t, 1)], ACT.Sqrt).then_inc(root_ready, 1)

            def quantise(t):
                quantise_u8(t)
                centre(t)

            def quantise_u8(t):
                p = t % 2
                act.wait_ge(ln1_ready, t + 1)
                nc.scalar.activation(q1_u8[:, bass.ds(p, 1), :], x_all[:, bass.ds(t, 1), :], ACT.Identity,
                                     scale=scale1[:, bass.ds(t, 1)], bias=shift1[:, bass.ds(t, 1)]).then_inc(q1_ready, 1)

            def centre(t):
                p = t % 2
                act.wait_ge(q1_ready, t + 1)
                nc.scalar.activation(a1[:, bass.ds(p, 1), :], q1_u8[:, bass.ds(p, 1), :], ACT.Identity, bias=neg_zi1,
                                     accum_out=a1_sum[:, bass.ds(t, 1)]).then_inc(a1_ready, 1)

            def copy_a1T(t):
                act.wait_ge(t1_done, t + 1)
                nc.scalar.copy(a1T[:, bass.ds(t % 2, 1), :, :].rearrange("p a k m -> p (a k m)"), p_t1[:, :]).then_inc(a1T_ready, 1)

            def copy_x2T(t, h):
                act.wait_ge(t2_done, 2 * t + h + 1)
                nc.scalar.copy(x2T[:, bass.ds(t % 2, 1), 4 * h:4 * h + 4, :].rearrange("p a k m -> p (a k m)"), p_t2[:, h, :]).then_inc(x2T_ready, 1)

            def square(t, buffer=None):
                act.wait_ge(mean2_ready, t + 1)
                nc.scalar.activation(squares[:, :], x2[:, bass.ds(t if buffer is None else buffer, 1), :].rearrange("p a n -> p (a n)"), ACT.Square,
                                     bias=ln2[:, NMEAN, bass.ds(t, 1)], accum_out=ln2[:, SQSUM, bass.ds(t, 1)]).then_inc(sq_ready, 1)

            def copy_whT(t):
                act.wait_ge(t3_done, t + 1)
                nc.scalar.copy(whT_hi[:, :], p_whT).then_inc(whT_hi_ready, 1)

            act.dma_start(given[:, :], given_in.rearrange("(a b) -> a b", a=1).broadcast_to([P, 4])).then_inc(given_landed, 16)
            ln1_root(0)
            act.wait_ge(fixed_ready, 1)
            quantise(0)
            ln1_root(1)
            copy_a1T(0)
            quantise_u8(1)
            centre(1)
            copy_a1T(1)
            ln1_root(2)
            quantise(2)
            act.wait_ge(main_done, 2)
            copy_a1T(2)
            copy_x2T(0, 0)
            copy_x2T(0, 1)
            ln1_root(3)
            act.wait_ge(b_landed, 16)
            nc.scalar.copy(b_hi[:, :], bT[:, :]).then_inc(b_hi_ready, 1)
            square(0)
            quantise(3)
            ln1_root(4)
            copy_x2T(1, 0)
            copy_x2T(1, 1)
            copy_whT(0)
            act.wait_ge(main_done, 4)
            copy_a1T(3)
            square(1)
            quantise(4)

            def period(t, buffer):
                act.wait_ge(s3_done, 2 * t - 4)
                copy_x2T(t - 1, 0)
                copy_whT(t - 2)
                copy_x2T(t - 1, 1)
                square(t - 1, buffer)
                ln1_root(t + 2)
                act.wait_ge(main_done, 2 * t)
                copy_a1T(t + 1)
                quantise(t + 2)

            with act.Fori(3, 6) as t:
                period(t, 1 + t % 2)
            for t in (6, 7):
                act.wait_ge(s3_done, 2 * t - 4)
                copy_x2T(t - 1, 0)
                copy_whT(t - 2)
                copy_x2T(t - 1, 1)
                square(t - 1, 1 + t % 2)
                if t == 6:
                    act.wait_ge(main_done, 12)
                    copy_a1T(7)
            copy_x2T(7, 0)
            act.wait_ge(sq_ready, 7)
            square(7, 0)
            copy_x2T(7, 1)
            act.wait_ge(s3_done, 12)
            copy_whT(6)
            act.wait_ge(s3_done, 14)
            copy_whT(7)

        @block.vector
        def _(dve):
            class Steps:
                n = 0

            def link(ins):
                Steps.n += 1
                ins.then_inc(dve_step, 1)
                dve.wait_ge(dve_step, Steps.n)

            def mark(ins):
                Steps.n += 1
                ins.then_inc(dve_step, 1)

            def seen():
                dve.wait_ge(dve_step, Steps.n)

            tt, ts, stt = nc.vector.tensor_tensor, nc.vector.tensor_scalar, nc.vector.scalar_tensor_tensor

            dve.wait_ge(given_landed, 16)
            nc.vector.reciprocal(r_s1, g_s1)
            nc.vector.tensor_copy(zi_u8[:, :], g_z1)
            link(tt(s12, g_s1, g_s2, ALU.mult))
            nc.vector.reciprocal(r_s2, g_s2)
            nc.vector.tensor_copy(zi1, zi_u8[:, :])
            link(ts(neg_zi1, zi_u8[:, :], -1.0, None, ALU.mult))
            tt(f1, g_z1, zi1, ALU.subtract)
            stt(out=neg_s12z2, in0=s12, scalar=-1.0, in1=g_z2, op0=ALU.mult, op1=ALU.mult).then_inc(fixed_ready, 1)

            def half_stats(t, h):
                return nc.vector.bn_stats(stats[:, 6 * h:6 * h + 6], x_all[:, bass.ds(t, 1), H * h:H * h + H].rearrange("p a d -> p (a d)"))

            def mean_and_var(t):
                link(nc.vector.bn_aggr(mean_var[:, :], stats[:, :]))
                ts(ln1[:, MEAN, bass.ds(t, 1)], mean_var[:, 0:1], 1.0, None, ALU.mult)
                link(ts(ln1[:, VAR, bass.ds(t, 1)], mean_var[:, 1:2], EPS, None, ALU.add))
                nc.vector.reciprocal(ln1[:, INV, bass.ds(t, 1)], ln1[:, VAR, bass.ds(t, 1)]).then_inc(inv1_ready, 1)

            def ln1_stats(t):
                dve.wait_ge(x_in[t % 2], 16 * (t // 2 + 1))
                half_stats(t, 0)
                link(half_stats(t, 1))
                mean_and_var(t)

            def newton_0():
                def c(i):
                    return ln1[:, i, 0:1]
                dve.wait_ge(root_ready, 1)
                link(tt(c(E1), c(ROOT), c(ROOT), ALU.mult))
                link(tt(c(E2), c(E1), c(VAR), ALU.mult))
                link(ts(c(E3), c(E2), -0.5, 1.5, ALU.mult, ALU.add))
                link(ts(scale1[:, 0:1], c(E3), c(ROOT), r_s1, ALU.mult, ALU.mult))
                link(ts(c(NSCALE), scale1[:, 0:1], -1.0, None, ALU.mult))
                ts(shift1[:, 0:1], c(NSCALE), c(MEAN), g_z1, ALU.mult, ALU.add).then_inc(ln1_ready, 1)

            def round_clip(b, k, r, done):
                link(ts(ctx_r[:, r, :], ctx_f[:, b, k, :], r_s2, g_z2, ALU.mult, ALU.add))
                ts(q2[:, b * K + k, :], ctx_r[:, r, :], QMAX, 0.0, ALU.min, ALU.max).then_inc(done, 1)

            def finish_clip(n):
                b, k = POOL_ROUNDS[n]
                dve.wait_ge(pool_rounded, n + 1)
                ts(q2[:, b * K + k, :], ctx_rp[:, n % 4, :], QMAX, 0.0, ALU.min, ALU.max).then_inc(q2_ready, 1)

            dve.wait_ge(x0_half, 16)
            half_stats(0, 0)
            dve.wait_ge(x_in[0], 16)
            link(half_stats(0, 1))
            mean_and_var(0)
            newton_0()
            ln1_stats(1)
            dve.wait_ge(ctx_sem[0], 16)
            round_clip(0, 0, 0, q2_ready)
            round_clip(0, 1, 1, q2_ready)
            dve.wait_ge(const_ready, 4)
            ts(k_f1, f1, float(D), None, ALU.mult)
            ts(flag[:, :], f1, 0.0, None, ALU.not_equal)
            link(ts(rest_f[:, 0, :], ones[:, :], f1, -1.0, ALU.mult, ALU.mult))
            link(nc.vector.tensor_copy(rest[:, 0, :], rest_f[:, 0, :]))
            link(tt(rest_f[:, 1, :], rest_f[:, 0, :], rest[:, 0, :], ALU.subtract))
            link(nc.vector.tensor_copy(rest[:, 1, :], rest_f[:, 1, :]))
            link(tt(rest_f[:, 0, :], rest_f[:, 1, :], rest[:, 1, :], ALU.subtract))
            nc.vector.tensor_copy(rest[:, 2, :], rest_f[:, 0, :]).then_inc(rest_ready, 1)
            dve.wait_ge(ctx_sem[1], 16)
            dve.wait_ge(q2_ready, 2)
            round_clip(0, 2, 0, q2_ready)
            finish_clip(0)
            dve.wait_ge(ctx_sem[2], 16)
            round_clip(0, 4, 1, q2_ready)
            finish_clip(1)
            ln1_stats(2)
            dve.wait_ge(ctx_sem[3], 16)
            dve.wait_ge(q2_ready, 3)
            round_clip(0, 6, 0, q2_ready)
            dve.wait_ge(q2_ready, 5)
            round_clip(0, 7, 1, q2_ready)

            def col(i, t):
                return ln2[:, i, bass.ds(t, 1)]

            def half(buffer, h):
                return x2[:, bass.ds(buffer, 1), H * h:H * h + H].rearrange("p a d -> p (a d)")

            def join_main(t, h, buffer, product=p_main):
                dve.wait_ge(main_done, 2 * t + h + 1)
                stt(out=half(buffer, h), in0=product[:, h, :], scalar=s12,
                    in1=x_all[:, bass.ds(t, 1), H * h:H * h + H].rearrange("p a d -> p (a d)"), op0=ALU.mult, op1=ALU.add,
                    accum_out=col(SUM0 + h, t)).then_inc(x2_ready, 1)

            def mean2(t):
                dve.wait_ge(x2_ready, 2 * t + 2)
                ts(col(NMEAN, t), col(SUM0, t), col(SUM1, t), -1.0 / N, ALU.add, ALU.mult).then_inc(mean2_ready, 1)

            def offset(t):
                ts(col(U, t), a1_sum[:, bass.ds(t, 1)], k_f1, neg_s12z2, ALU.subtract, ALU.mult)

            def pick(t, p_s2=p_s2):
                dve.wait_ge(sq_ready, t + 1)
                link(ts(col(VAR2, t), col(SQSUM, t), 1.0 / N, EPS, ALU.mult, ALU.add))
                dve.wait_ge(s2_done, t + 1)
                dve.wait_ge(mean2_ready, t + 1)
                link(stt(out=lh[:, 0, :], in0=w_sum[:, :], scalar=col(NMEAN, t), in1=p_s2[:, 0:W], op0=ALU.mult, op1=ALU.add))
                mark(nc.vector.reciprocal(col(INV2, t), col(VAR2, t)))
                link(nc.vector.max(top8[:, :], lh[:, 0, 0:E]))
                mark(ts(col(COEF, t), top8[:, 0:1], col(INV2, t), None, ALU.mult))
                link(nc.vector.max_index(top_at[:, :], top8[:, :], lh[:, 0, 0:E]))
                mark(stt(out=lh[:, 1, E:W], in0=expert[:, :], scalar=top_at[:, 0:1], in1=lh[:, 0, E:W], op0=ALU.is_equal, op1=ALU.mult))

            def weigh(t):
                seen()
                ts(wh[:, :], lh[:, 1, E:W], col(COEF, t), None, ALU.mult).then_inc(wh_ready, 1)

            def split_whT(t):
                dve.wait_ge(whT_hi_ready, t + 1)
                tt(whT_lo[:, :], p_whT, whT_hi[:, :].bitcast(F32), ALU.subtract).then_inc(whT_ready, 1)

            def finish(t, buffer, halves=(0, 1), product=p_s3):
                for h in halves:
                    dve.wait_ge(s3_done, 2 * t + h + 1)
                    stt(out=x_all[:, bass.ds(t, 1), H * h:H * h + H].rearrange("p a d -> p (a d)"), in0=product[:, h, :], scalar=col(U, t),
                        in1=half(buffer, h), op0=ALU.add, op1=ALU.add).then_inc(res_ready, 1)

            join_main(0, 0, 0)
            join_main(0, 1, 0)
            mean2(0)
            offset(0)
            ln1_stats(3)
            dve.wait_ge(w_sum_done, 1)
            nc.vector.tensor_copy(w_sum[:, :], p_s2[:, 0:W]).then_inc(w_sum_ready, 1)
            join_main(1, 0, 1, p_s3)
            join_main(1, 1, 1, p_s3)
            mean2(1)
            offset(1)
            ln1_stats(4)
            dve.wait_ge(w_sum_ready, 1)
            pick(0)
            weigh(0)
            join_main(2, 0, 2)
            split_whT(0)
            dve.wait_ge(b_hi_ready, 1)
            tt(b_lo[:, :], bT[:, :], b_hi[:, :].bitcast(F32), ALU.subtract).then_inc(b_lo_ready, 1)
            join_main(2, 1, 2)
            mean2(2)
            finish_clip(2)
            finish_clip(3)
            finish_clip(4)
            finish_clip(5)
            pick(1)
            weigh(1)
            finish(0, 0)

            def period(t, p, finished, more=True):
                if more and t > 3:
                    half_stats(t + 2, 0)
                split_whT(t - 2)
                if t == 3:
                    finish_clip(6)
                    finish_clip(7)
                    half_stats(5, 0)
                if more:
                    link(half_stats(t + 2, 1))
                    mean_and_var(t + 2)
                offset(t - 1)
                finish(t - 2, finished)
                dve.wait_ge(res_ready, 2 * t - 2)
                join_main(t, 0, p)
                if t == 3:
                    finish_clip(8)
                    finish_clip(9)
                pick(t - 1)
                join_main(t, 1, p)
                weigh(t - 1)
                mean2(t)

            dve.wait_ge(x_in[1], 48)
            period(3, 1, 1)
            dve.wait_ge(x_in[0], 64)
            dve.wait_ge(x_in[1], 64)
            period(4, 2, 2)
            period(5, 1, 1)
            period(6, 2, 2, more=False)
            split_whT(5)
            offset(6)
            join_main(7, 0, 0)
            finish(5, 1)
            join_main(7, 1, 0)
            mean2(7)
            offset(7)
            pick(6)
            weigh(6)
            split_whT(6)
            pick(7, p_main[:, 0, :])
            weigh(7)
            finish(6, 2, (0,))
            split_whT(7)
            finish(6, 2, (1,))
            finish(7, 0, product=p_main)

        @block.tensor
        def _(pe):
            def transpose_a1(t, p):
                pe.wait_ge(a1_ready, t + 1)
                pe.wait_ge(a1T_ready, t)
                for k in range(K):
                    last = nc.tensor.transpose(p_t1[:, P * k:P * k + P], a1[:, p, P * k:P * k + P], ident_b[:, :])
                last.then_inc(t1_done, 1)

            def product(out, b, p, h, k):
                return nc.tensor.matmul(out[:, h, :], a1T[:, p, k, :], q2[:, bass.ds(b * K + k, 1), H * h:H * h + H].rearrange("p a n -> p (a n)"),
                                        start=(k == 0), stop=(k == K - 1))

            def add_rest(out, b, h):
                with nc.tensor.If(has_rest != 0):
                    for k in range(K):
                        for part in range(3):
                            nc.tensor.matmul(out[:, h, :], rest[:, part, :], q2[:, bass.ds(b * K + k, 1), H * h:H * h + H].rearrange("p a n -> p (a n)"),
                                             start=False, stop=False)

            def main(b, p, h, k0, k1):
                for k in range(k0, k1):
                    if k == K - 1:
                        add_rest(p_main, b, h)
                    last = product(p_main, b, p, h, k)
                if k1 == K:
                    last.then_inc(main_done, 1)

            def transpose_x2(t, p, halves=(0, 1)):
                for h in halves:
                    pe.wait_ge(x2_ready, 2 * t + h + 1)
                    for k in range(4 * h, 4 * h + 4):
                        last = nc.tensor.transpose(p_t2[:, h, P * (k % 4):P * (k % 4) + P], x2[:, p, P * k:P * k + P], ident[:, :])
                    last.then_inc(t2_done, 1)

            def logits_and_h(t, p, p_s2=p_s2, ks=range(K)):
                for k in ks:
                    if k % 4 == 0:
                        pe.wait_ge(x2T_ready, 2 * t + k // 4 + 1)
                    last = nc.tensor.matmul(p_s2[:, 0:W], x2T[:, p, k, :], wT[:, k, :], start=(k == 0), stop=(k == K - 1))
                if k == K - 1:
                    last.then_inc(s2_done, 1)

            def transpose_wh(t):
                pe.wait_ge(wh_ready, t + 1)
                nc.tensor.transpose(p_whT, wh[:, :], ident[:, :]).then_inc(t3_done, 1)

            def lora_out(t, out=p_s3):
                pe.wait_ge(whT_ready, t + 1)
                for h in range(2):
                    n = slice(H * h, H * h + H)
                    nc.tensor.matmul(out[:, h, :], whT_hi[:, :], b_hi[:, n], start=True, stop=False)
                    nc.tensor.matmul(out[:, h, :], whT_hi[:, :], b_lo[:, n], start=False, stop=False)
                    nc.tensor.matmul(out[:, h, :], whT_lo[:, :], b_hi[:, n], start=False, stop=True).then_inc(s3_done, 1)

            pe.wait_ge(const_ready, 4)
            transpose_a1(0, 0)
            pe.wait_ge(a1T_ready, 1)
            for k in range(4):
                pe.wait_ge(q2_ready, k + 1)
                for h in range(2):
                    product(p_main, 0, 0, h, k)
                if k == 1:
                    transpose_a1(1, 1)
            pe.wait_ge(a1T_ready, 2)
            for k in range(4):
                for h in range(2):
                    product(p_s3, 0, 1, h, k)
            pe.wait_ge(rest_ready, 1)
            has_rest = pe.value_load(flag[0:1, 0:1], min_val=0, max_val=1)
            for k in range(4, K):
                pe.wait_ge(q2_ready, k + 1)
                for p, out in enumerate((p_main, p_s3)):
                    for h in range(2):
                        if k == K - 1:
                            add_rest(out, 0, h)
                        last = product(out, 0, p, h, k)
                        if k == K - 1:
                            last.then_inc(main_done, 1)
            transpose_a1(2, 0)
            pe.wait_ge(w_folded, 1)
            nc.tensor.matmul(p_s2[:, 0:W], ones[:, :], w_fold[:, 6, :], start=True, stop=True).then_inc(w_sum_done, 1)
            transpose_x2(0, 0)
            pe.wait_ge(a1T_ready, 3)
            main(0, 0, 0, 0, K)
            pe.wait_ge(w_sum_ready, 1)
            logits_and_h(0, 0)
            pe.wait_ge(x2T_ready, 2)
            transpose_x2(1, 1)
            main(0, 0, 1, 0, 4)
            transpose_a1(3, 1)
            transpose_wh(0)
            main(0, 0, 1, 4, K)
            pe.wait_ge(whT_ready, 1)
            logits_and_h(1, 1)
            pe.wait_ge(b_lo_ready, 1)
            lora_out(0)

            def period(t, p, b, x2_buffer, more=True):
                pe.wait_ge(a1T_ready, t + 1)
                pe.wait_ge(x2_ready, 2 * t - 1)
                main(b, p, 0, 0, K - 2)
                if p == 0:
                    pe.wait_ge(q2_ready, 2 * K)
                main(b, p, 0, K - 2, K)
                pe.wait_ge(x2T_ready, 2 * t - 2)
                transpose_x2(t - 1, x2_buffer)
                transpose_wh(t - 2)
                main(b, p, 1, 0, 4)
                pe.wait_ge(res_ready, 2 * t - 4)
                lora_out(t - 2)
                if more:
                    transpose_a1(t + 1, 1 - p)
                    logits_and_h(t - 1, 1 - p)
                main(b, p, 1, 4, K)

            with pe.Fori(0, 2) as i:
                period(2 * i + 3, 1, i, 2)
                pe.wait_ge(q2_ready, 2 * K - 2)
                period(2 * i + 4, 0, 1, 1)
            period(7, 1, 1, 2, more=False)
            pe.wait_ge(x2T_ready, 14)
            transpose_x2(7, 0, (0,))
            logits_and_h(6, 0)
            transpose_x2(7, 0, (1,))
            logits_and_h(7, 1, p_main[:, 0, :], range(4))
            transpose_wh(6)
            logits_and_h(7, 1, p_main[:, 0, :], range(4, K))
            pe.wait_ge(res_ready, 12)
            lora_out(6)
            transpose_wh(7)
            lora_out(7, p_main)


def kernel(**inputs):
    import numpy as _np
    import concourse.bacc as _bacc
    from concourse import mybir as _mybir
    from concourse.bass_utils import run_bass_kernel_spmd as _run

    a = {k: _np.asarray(v) for k, v in inputs.items()}
    experts, rank, d = a["L0_ffn_A"].shape
    k = d // 128
    w = _np.concatenate([a["L0_ffn_route_w"].T, a["L0_ffn_A"].reshape(experts * rank, d).T], axis=1)
    arrays = {
        "x": a["x"],
        "ctx": a["ctx_4096"],
        "given": _np.concatenate([a["L0_xattn_x1_scale"], a["L0_xattn_x1_zp"], a["L0_xattn_x2_scale"], a["L0_xattn_x2_zp"]]),
        "down": w.reshape(k, 128, w.shape[1]).transpose(1, 0, 2).reshape(128, k * w.shape[1]),
        "up": a["L0_ffn_Bw"].transpose(0, 2, 1).reshape(experts * rank, -1),
    }
    arrays = {f"in_{n}_dram": _np.ascontiguousarray(v) for n, v in arrays.items()}
    nc = _bacc.Bacc("TRN2", target_bir_lowering=False, num_devices=1)
    args = [nc.dram_tensor(n, v.shape, _mybir.dt.from_np(v.dtype), kind="ExternalInput").ap() for n, v in arrays.items()]
    args.append(nc.dram_tensor("out_0_dram", (2, 512, 1024), _mybir.dt.from_np(_np.dtype("float32")), kind="ExternalOutput").ap())
    build(nc, *args)
    return _run(nc, [arrays], core_ids=[0]).results[0]["out_0_dram"]
```

```python
from contextlib import ExitStack

import concourse.bass as bass
from concourse import mybir

ALU = mybir.AluOpType
ACT = mybir.ActivationFunctionType
F32 = mybir.dt.float32
BF16 = mybir.dt.bfloat16
I16 = mybir.dt.int16
F32R = mybir.dt.float32r
U8 = mybir.dt.uint8
U32 = mybir.dt.uint32
I32 = mybir.dt.int32

P = 128
EPS = 1e-5
QMAX = 255.0


def build(nc, x, ctx_in, given_in, w_in, b_in, out):
    B, S, D = x.shape
    N = ctx_in.shape[2]
    ER = b_in.shape[0]
    T = B * S // P
    K = D // P
    H = 512
    W = w_in.shape[1] // K
    E = W - ER
    R = ER // E
    assert ER == P and N == 2 * H and D == N and T == 8 and K == 8 and B == 2 and E == 8

    x_dram = x.rearrange("b s d -> (b s) d").rearrange("(t p) d -> t p d", p=P)
    out_dram = out.rearrange("b s d -> (b s) d").rearrange("(t p) d -> t p d", p=P)
    ctx_dram = ctx_in.rearrange("b (j c p) n -> b j p c n", p=P, c=2)

    with ExitStack() as stack:
        def sb(name, shape, dt):
            return stack.enter_context(nc.sbuf_tensor(name, shape, dt))

        def bank(name, shape, dt):
            return stack.enter_context(nc.psum_tensor(name, shape, dt))

        def sem(name):
            return stack.enter_context(nc.semaphore(name))

        x_all = sb("x_all", [P, T, D], F32)
        ctx_f = sb("ctx_f", [P, B, K, N], F32)
        ctx_r = sb("ctx_r", [P, 2, N], I16)
        ctx_rp = sb("ctx_rp", [P, 4, N], I16)
        q2 = sb("q2", [P, B * K, N], BF16)
        q1_u8 = sb("q1_u8", [P, 2, D], U8)
        a1 = sb("a1", [P, 2, D], BF16)
        a1T = sb("a1T", [P, 2, K, P], BF16)
        x2 = sb("x2", [P, 3, N], F32)
        x2T = sb("x2T", [P, 2, K, P], F32)
        squares = sb("squares", [P, N], BF16)
        wT = sb("wT", [P, K, W], F32)
        bT = sb("bT", [P, N], F32)
        b_hi = sb("b_hi", [P, N], F32R)
        b_lo = sb("b_lo", [P, N], F32R)
        w_fold = sb("w_fold", [P, 7, W], F32)
        w_sum = sb("w_sum", [P, W], F32)
        lh = sb("lh", [P, 2, W], F32)
        wh = sb("wh", [P, ER], F32)
        whT_hi = sb("whT_hi", [P, P], F32R)
        whT_lo = sb("whT_lo", [P, P], F32R)
        ident = sb("ident", [P, P], F32)
        ident_b = sb("ident_b", [P, P], BF16)
        ones = sb("ones", [P, P], F32)
        expert = sb("expert", [P, ER], F32)
        stats = sb("stats", [P, 12], F32)
        mean_var = sb("mean_var", [P, 2], F32)
        ln1 = sb("ln1", [P, 8, T], F32)
        scale1 = sb("scale1", [P, T], F32)
        shift1 = sb("shift1", [P, T], F32)
        a1_sum = sb("a1_sum", [P, T], F32)
        ln2 = sb("ln2", [P, 8, T], F32)
        top8 = sb("top8", [P, 8], F32)
        top_at = sb("top_at", [P, 8], U32)
        given = sb("given", [P, 4], F32)
        zi_u8 = sb("zi_u8", [P, 1], U8)
        fixed = sb("fixed", [P, 8], F32)
        rest = sb("rest", [P, 3, P], BF16)
        rest_f = sb("rest_f", [P, 2, P], F32)
        flag = sb("flag", [P, 1], I32)
        g_s1, g_z1, g_s2, g_z2 = (given[:, i:i + 1] for i in range(4))
        r_s1, r_s2, zi1, neg_zi1, f1, k_f1, s12, neg_s12z2 = (fixed[:, i:i + 1] for i in range(8))
        MEAN, VAR, INV, ROOT, E1, E2, E3, NSCALE = range(8)
        SUM0, SUM1, NMEAN, SQSUM, VAR2, INV2, COEF, U = range(8)

        p_t1 = bank("p_t1", [P, K * P], BF16)
        p_main = bank("p_main", [P, 2, H], F32)
        p_t2 = bank("p_t2", [P, 2, H], F32)
        p_s2 = bank("p_s2", [P, H], F32)
        p_s3 = bank("p_s3", [P, 2, H], F32)
        p_whT = p_s2[:, 256:256 + P]

        given_landed = sem("given_landed")
        x0_half = sem("x0_half")
        x_in = [sem(f"x_in{i}") for i in range(2)]
        ctx_sem = [sem(f"ctx_in{j}") for j in range(K // 2)]
        w_landed, b_landed = sem("w_landed"), sem("b_landed")
        const_set, const_ready = sem("const_set"), sem("const_ready")
        fixed_ready, rest_ready = sem("fixed_ready"), sem("rest_ready")
        dve_step, pool_step = sem("dve_step"), sem("pool_step")
        inv1_ready, root_ready, ln1_ready = sem("inv1_ready"), sem("root_ready"), sem("ln1_ready")
        q1_ready, a1_ready, t1_done, a1T_ready = sem("q1_ready"), sem("a1_ready"), sem("t1_done"), sem("a1T_ready")
        pool_rounded, q2_ready = sem("pool_rounded"), sem("q2_ready")
        main_done, x2_ready, t2_done, x2T_ready = sem("main_done"), sem("x2_ready"), sem("t2_done"), sem("x2T_ready")
        mean2_ready, sq_ready = sem("mean2_ready"), sem("sq_ready")
        s2_done, wh_ready, t3_done = sem("s2_done"), sem("wh_ready"), sem("t3_done")
        whT_hi_ready, whT_ready = sem("whT_hi_ready"), sem("whT_ready")
        s3_done, res_ready = sem("s3_done"), sem("res_ready")
        out_stored = [sem(f"out_stored{i}") for i in range(2)]
        last_stored = [sem(f"last_stored{i}") for i in range(4)]
        w_folded = sem("w_folded")
        w_sum_done, w_sum_ready, b_hi_ready, b_lo_ready = sem("w_sum_done"), sem("w_sum_ready"), sem("b_hi_ready"), sem("b_lo_ready")

        block = stack.enter_context(nc.Block())
        POOL_ROUNDS = tuple((0, k) for k in range(1, K, 2)) + tuple((1, k) for k in range(K))
        READ_AT = tuple(b * K + k + 1 for b, k in POOL_ROUNDS)

        @block.sync
        def _(sp):
            def load_x(t):
                if t >= 2:
                    sp.wait_ge(x_in[t % 2], 16 * (t // 2))
                sp.dma_start(x_all[:, t, :], x_dram[t]).then_inc(x_in[t % 2], 16)

            def load_ctx(b, j):
                if b:
                    sp.wait_ge(ctx_sem[j], 16)
                sp.dma_start(ctx_f[:, b, 2 * j:2 * j + 2, :], ctx_dram[b, j]).then_inc(ctx_sem[j], 16)

            sp.dma_start(x_all[:, 0, 0:H], x_dram[0][:, 0:H]).then_inc(x0_half, 16)
            sp.dma_start(x_all[:, 0, H:D], x_dram[0][:, H:D]).then_inc(x_in[0], 16)
            load_x(1)
            for j in range(3):
                load_ctx(0, j)
            load_x(2)
            load_ctx(0, 3)
            sp.dma_start(wT[:, :, :], w_in.rearrange("p (k w) -> p k w", w=W)).then_inc(w_landed, 16)
            sp.dma_start(bT[:, :], b_in).then_inc(b_landed, 16)
            load_x(3)
            load_x(4)
            for j in range(3):
                load_ctx(1, j)
            load_x(5)
            load_ctx(1, 3)
            load_x(6)
            load_x(7)

            def transpose_a1(t, p):
                sp.wait_ge(a1_ready, t + 1)
                sp.wait_ge(main_done, 2 * t - 2)
                sp.wait_ge(a1T_ready, 16 * t)
                sp.dma_start_transpose(a1T[:, p, :, :], a1[:, p, :]).then_inc(a1T_ready, 16)

            def store(t, p):
                sp.wait_ge(res_ready, 2 * t + 2)
                sp.dma_start(out_dram[bass.ds(t, 1)].rearrange("a p d -> p a d"), x_all[:, bass.ds(t, 1), :]).then_inc(out_stored[p], 16)

            transpose_a1(4, 0)
            store(0, 0)
            transpose_a1(5, 1)
            store(1, 1)
            transpose_a1(6, 0)
            store(2, 0)
            transpose_a1(7, 1)
            store(3, 1)
            store(4, 0)
            store(5, 1)
            for t in range(T - 2, T):
                for h in range(2):
                    sp.wait_ge(res_ready, 2 * t + h + 1)
                    sp.dma_start(out_dram[t][:, H * h:H * h + H], x_all[:, t, H * h:H * h + H]).then_inc(last_stored[2 * (t % 2) + h], 16)
            for h in range(2):
                sp.wait_ge(out_stored[h], 16 * (T // 2 - 1))
            for stored in last_stored:
                sp.wait_ge(stored, 16)

        @block.gpsimd
        def _(pool):
            steps = [0]

            def link(ins):
                steps[0] += 1
                ins.then_inc(pool_step, 1)
                pool.wait_ge(pool_step, steps[0])

            nc.gpsimd.memset(ident_b[:, :], 0.0).then_inc(const_set, 1)
            nc.gpsimd.memset(ident[:, :], 0.0).then_inc(const_set, 1)
            for n, m in enumerate((ident_b, ident)):
                pool.wait_ge(const_set, n + 1)
                nc.gpsimd.affine_select(out=m[:, :], in_=m[:, :], compare_op=ALU.not_equal, fill=1.0, base=0,
                                        pattern=[[-1, P]], channel_multiplier=1).then_inc(const_ready, 1)
            nc.gpsimd.memset(ones[:, :], 1.0).then_inc(const_ready, 1)
            nc.gpsimd.iota(expert[:, :], [[1, E], [0, R]], base=0, channel_multiplier=0,
                           allow_small_or_imprecise_dtypes=True).then_inc(const_ready, 1)

            def ln1_finish(t):
                def col(i):
                    return ln1[:, i, t:t + 1]
                pool.wait_ge(root_ready, t + 1)
                link(nc.gpsimd.tensor_tensor(col(E1), col(ROOT), col(ROOT), ALU.mult))
                link(nc.gpsimd.tensor_tensor(col(E2), col(E1), col(VAR), ALU.mult))
                link(nc.gpsimd.tensor_scalar(col(E3), col(E2), 0.5, -1.5, ALU.mult, ALU.add))
                link(nc.gpsimd.tensor_scalar(col(NSCALE), col(E3), col(ROOT), r_s1, ALU.mult, ALU.mult))
                nc.gpsimd.tensor_scalar(scale1[:, t:t + 1], col(NSCALE), -1.0, 1.0, ALU.mult, ALU.mult)
                nc.gpsimd.tensor_scalar(shift1[:, t:t + 1], col(NSCALE), col(MEAN), g_z1,
                                        ALU.mult, ALU.add).then_inc(ln1_ready, 1)

            def round_ctx(n):
                b, k = POOL_ROUNDS[n]
                pool.wait_ge(ctx_sem[k // 2], 16 * (b + 1))
                if n >= 4:
                    pool.wait_ge(q2_ready, READ_AT[n - 4])
                nc.gpsimd.tensor_scalar(ctx_rp[:, n % 4, :], ctx_f[:, b, k, :], r_s2, g_z2, ALU.mult, ALU.add).then_inc(pool_rounded, 1)

            pool.wait_ge(fixed_ready, 1)
            round_ctx(0)
            pool.wait_ge(ln1_ready, 1)
            ln1_finish(1)
            round_ctx(1)
            round_ctx(2)
            round_ctx(3)
            pool.wait_ge(w_landed, 16)
            link(nc.gpsimd.tensor_tensor(w_fold[:, 0:4, :], wT[:, 0:4, :], wT[:, 4:8, :], ALU.add))
            link(nc.gpsimd.tensor_tensor(w_fold[:, 4:6, :], w_fold[:, 0:2, :], w_fold[:, 2:4, :], ALU.add))
            nc.gpsimd.tensor_tensor(w_fold[:, 6, :], w_fold[:, 4, :], w_fold[:, 5, :], ALU.add).then_inc(w_folded, 1)
            pool.wait_ge(b_hi_ready, 1)
            nc.gpsimd.tensor_tensor(b_lo[:, :], bT[:, :], b_hi[:, :].bitcast(F32), ALU.subtract).then_inc(b_lo_ready, 1)
            pool.wait_ge(ln1_ready, 3)
            ln1_finish(3)
            for n in range(4, 4 + K):
                round_ctx(n)
                if n == 7:
                    ln1_finish(4)
            ln1_finish(5)
            ln1_finish(6)
            ln1_finish(7)

        @block.scalar
        def _(act):
            def ln1_root(t):
                act.wait_ge(inv1_ready, t + 1)
                nc.scalar.activation(ln1[:, ROOT, bass.ds(t, 1)], ln1[:, INV, bass.ds(t, 1)], ACT.Sqrt).then_inc(root_ready, 1)

            def quantise(t):
                quantise_u8(t)
                centre(t)

            def quantise_u8(t):
                p = t % 2
                act.wait_ge(ln1_ready, t + 1)
                nc.scalar.activation(q1_u8[:, bass.ds(p, 1), :], x_all[:, bass.ds(t, 1), :], ACT.Identity,
                                     scale=scale1[:, bass.ds(t, 1)], bias=shift1[:, bass.ds(t, 1)]).then_inc(q1_ready, 1)

            def centre(t):
                p = t % 2
                act.wait_ge(q1_ready, t + 1)
                nc.scalar.activation(a1[:, bass.ds(p, 1), :], q1_u8[:, bass.ds(p, 1), :], ACT.Identity, bias=neg_zi1,
                                     accum_out=a1_sum[:, bass.ds(t, 1)]).then_inc(a1_ready, 1)

            def copy_a1T(t):
                act.wait_ge(t1_done, t + 1)
                nc.scalar.copy(a1T[:, bass.ds(t % 2, 1), :, :].rearrange("p a k m -> p (a k m)"), p_t1[:, :]).then_inc(a1T_ready, 16)

            def copy_x2T(t, h):
                act.wait_ge(t2_done, 2 * t + h + 1)
                nc.scalar.copy(x2T[:, bass.ds(t % 2, 1), 4 * h:4 * h + 4, :].rearrange("p a k m -> p (a k m)"), p_t2[:, h, :]).then_inc(x2T_ready, 1)

            def square(t, buffer):
                act.wait_ge(mean2_ready, t + 1)
                nc.scalar.activation(squares[:, :], x2[:, bass.ds(buffer, 1), :].rearrange("p a n -> p (a n)"), ACT.Square,
                                     bias=ln2[:, NMEAN, bass.ds(t, 1)], accum_out=ln2[:, SQSUM, bass.ds(t, 1)]).then_inc(sq_ready, 1)

            def copy_whT(t):
                act.wait_ge(t3_done, t + 1)
                nc.scalar.copy(whT_hi[:, :], p_whT).then_inc(whT_hi_ready, 1)

            act.dma_start(given[:, :], given_in.rearrange("(a b) -> a b", a=1).broadcast_to([P, 4])).then_inc(given_landed, 16)
            ln1_root(0)
            act.wait_ge(fixed_ready, 1)
            quantise(0)
            ln1_root(1)
            copy_a1T(0)
            quantise(1)
            copy_a1T(1)
            ln1_root(2)
            quantise(2)
            act.wait_ge(b_landed, 16)
            nc.scalar.copy(b_hi[:, :], bT[:, :]).then_inc(b_hi_ready, 1)
            act.wait_ge(main_done, 2)
            copy_a1T(2)
            copy_x2T(0, 0)
            copy_x2T(0, 1)
            ln1_root(3)
            square(0, 0)
            quantise_u8(3)
            copy_x2T(1, 0)
            copy_x2T(1, 1)
            copy_whT(0)
            centre(3)
            act.wait_ge(sq_ready, 1)
            square(1, 1)
            ln1_root(4)
            act.wait_ge(main_done, 4)
            copy_a1T(3)
            quantise(4)

            def period(t, buffer):
                act.wait_ge(s3_done, 2 * t - 4)
                copy_x2T(t - 1, 0)
                copy_whT(t - 2)
                copy_x2T(t - 1, 1)
                square(t - 1, buffer)
                ln1_root(t + 2)
                quantise(t + 2)

            with act.Fori(3, 6) as t:
                period(t, 1 + t % 2)
            for t in (6, 7):
                act.wait_ge(s3_done, 2 * t - 4)
                copy_x2T(t - 1, 0)
                copy_whT(t - 2)
                copy_x2T(t - 1, 1)
                square(t - 1, 1 + t % 2)
            act.wait_ge(sq_ready, 7)
            square(7, 0)
            copy_x2T(7, 0)
            copy_x2T(7, 1)
            act.wait_ge(s3_done, 12)
            copy_whT(6)
            act.wait_ge(s3_done, 14)
            copy_whT(7)

        @block.vector
        def _(dve):
            class Steps:
                n = 0

            def link(ins):
                Steps.n += 1
                ins.then_inc(dve_step, 1)
                dve.wait_ge(dve_step, Steps.n)

            def mark(ins):
                Steps.n += 1
                ins.then_inc(dve_step, 1)

            def seen():
                dve.wait_ge(dve_step, Steps.n)

            tt, ts, stt = nc.vector.tensor_tensor, nc.vector.tensor_scalar, nc.vector.scalar_tensor_tensor

            dve.wait_ge(given_landed, 16)
            nc.vector.reciprocal(r_s1, g_s1)
            nc.vector.tensor_copy(zi_u8[:, :], g_z1)
            link(tt(s12, g_s1, g_s2, ALU.mult))
            nc.vector.reciprocal(r_s2, g_s2)
            nc.vector.tensor_copy(zi1, zi_u8[:, :])
            link(ts(neg_zi1, zi_u8[:, :], -1.0, None, ALU.mult))
            tt(f1, g_z1, zi1, ALU.subtract)
            stt(out=neg_s12z2, in0=s12, scalar=-1.0, in1=g_z2, op0=ALU.mult, op1=ALU.mult).then_inc(fixed_ready, 1)

            def half_stats(t, h):
                return nc.vector.bn_stats(stats[:, 6 * h:6 * h + 6], x_all[:, bass.ds(t, 1), H * h:H * h + H].rearrange("p a d -> p (a d)"))

            def mean_and_var(t):
                link(nc.vector.bn_aggr(mean_var[:, :], stats[:, :]))
                ts(ln1[:, MEAN, bass.ds(t, 1)], mean_var[:, 0:1], 1.0, None, ALU.mult)
                link(ts(ln1[:, VAR, bass.ds(t, 1)], mean_var[:, 1:2], EPS, None, ALU.add))
                nc.vector.reciprocal(ln1[:, INV, bass.ds(t, 1)], ln1[:, VAR, bass.ds(t, 1)]).then_inc(inv1_ready, 1)

            def ln1_stats(t):
                dve.wait_ge(x_in[t % 2], 16 * (t // 2 + 1))
                half_stats(t, 0)
                link(half_stats(t, 1))
                mean_and_var(t)

            def ln1_newton(t):
                def c(i):
                    return ln1[:, i, t:t + 1]
                dve.wait_ge(root_ready, t + 1)
                link(tt(c(E1), c(ROOT), c(ROOT), ALU.mult))
                link(tt(c(E2), c(E1), c(VAR), ALU.mult))
                link(ts(c(E3), c(E2), -0.5, 1.5, ALU.mult, ALU.add))
                link(ts(scale1[:, t:t + 1], c(E3), c(ROOT), r_s1, ALU.mult, ALU.mult))
                link(ts(c(NSCALE), scale1[:, t:t + 1], -1.0, None, ALU.mult))
                ts(shift1[:, t:t + 1], c(NSCALE), c(MEAN), g_z1, ALU.mult, ALU.add).then_inc(ln1_ready, 1)

            def round_clip(b, k, r):
                link(ts(ctx_r[:, r, :], ctx_f[:, b, k, :], r_s2, g_z2, ALU.mult, ALU.add))
                ts(q2[:, b * K + k, :], ctx_r[:, r, :], QMAX, 0.0, ALU.min, ALU.max).then_inc(q2_ready, 1)

            def finish_clip(n):
                b, k = POOL_ROUNDS[n]
                dve.wait_ge(pool_rounded, n + 1)
                ts(q2[:, b * K + k, :], ctx_rp[:, n % 4, :], QMAX, 0.0, ALU.min, ALU.max).then_inc(q2_ready, 1)

            dve.wait_ge(x0_half, 16)
            half_stats(0, 0)
            dve.wait_ge(x_in[0], 16)
            link(half_stats(0, 1))
            mean_and_var(0)
            ln1_newton(0)
            ln1_stats(1)
            dve.wait_ge(ctx_sem[0], 16)
            round_clip(0, 0, 0)
            finish_clip(0)
            dve.wait_ge(const_ready, 4)
            ts(k_f1, f1, float(D), None, ALU.mult)
            ts(flag[:, :], f1, 0.0, None, ALU.not_equal)
            link(ts(rest_f[:, 0, :], ones[:, :], f1, -1.0, ALU.mult, ALU.mult))
            link(nc.vector.tensor_copy(rest[:, 0, :], rest_f[:, 0, :]))
            link(tt(rest_f[:, 1, :], rest_f[:, 0, :], rest[:, 0, :], ALU.subtract))
            link(nc.vector.tensor_copy(rest[:, 1, :], rest_f[:, 1, :]))
            link(tt(rest_f[:, 0, :], rest_f[:, 1, :], rest[:, 1, :], ALU.subtract))
            nc.vector.tensor_copy(rest[:, 2, :], rest_f[:, 0, :]).then_inc(rest_ready, 1)
            dve.wait_ge(ctx_sem[1], 16)
            round_clip(0, 2, 1)
            finish_clip(1)
            dve.wait_ge(ctx_sem[2], 16)
            dve.wait_ge(q2_ready, 1)
            round_clip(0, 4, 0)
            finish_clip(2)
            ln1_stats(2)
            dve.wait_ge(ln1_ready, 2)
            ln1_newton(2)
            dve.wait_ge(ctx_sem[3], 16)
            dve.wait_ge(q2_ready, 3)
            round_clip(0, 6, 1)
            finish_clip(3)

            def col(i, t):
                return ln2[:, i, bass.ds(t, 1)]

            def half(buffer, h):
                return x2[:, bass.ds(buffer, 1), H * h:H * h + H].rearrange("p a d -> p (a d)")

            def join_main(t, h, buffer, product=p_main):
                dve.wait_ge(main_done, 2 * t + h + 1)
                stt(out=half(buffer, h), in0=product[:, h, :], scalar=s12,
                    in1=x_all[:, bass.ds(t, 1), H * h:H * h + H].rearrange("p a d -> p (a d)"), op0=ALU.mult, op1=ALU.add,
                    accum_out=col(SUM0 + h, t)).then_inc(x2_ready, 1)

            def mean2(t):
                dve.wait_ge(x2_ready, 2 * t + 2)
                ts(col(NMEAN, t), col(SUM0, t), col(SUM1, t), -1.0 / N, ALU.add, ALU.mult).then_inc(mean2_ready, 1)

            def offset(t):
                ts(col(U, t), a1_sum[:, bass.ds(t, 1)], k_f1, neg_s12z2, ALU.subtract, ALU.mult)

            def pick(t, p_s2=p_s2):
                dve.wait_ge(sq_ready, t + 1)
                link(ts(col(VAR2, t), col(SQSUM, t), 1.0 / N, EPS, ALU.mult, ALU.add))
                dve.wait_ge(s2_done, t + 1)
                dve.wait_ge(mean2_ready, t + 1)
                link(stt(out=lh[:, 0, :], in0=w_sum[:, :], scalar=col(NMEAN, t), in1=p_s2[:, 0:W], op0=ALU.mult, op1=ALU.add))
                mark(nc.vector.reciprocal(col(INV2, t), col(VAR2, t)))
                link(nc.vector.max(top8[:, :], lh[:, 0, 0:E]))
                mark(ts(col(COEF, t), top8[:, 0:1], col(INV2, t), None, ALU.mult))
                link(nc.vector.max_index(top_at[:, :], top8[:, :], lh[:, 0, 0:E]))
                mark(stt(out=lh[:, 1, E:W], in0=expert[:, :], scalar=top_at[:, 0:1], in1=lh[:, 0, E:W], op0=ALU.is_equal, op1=ALU.mult))

            def weigh(t):
                seen()
                ts(wh[:, :], lh[:, 1, E:W], col(COEF, t), None, ALU.mult).then_inc(wh_ready, 1)

            def split_whT(t):
                dve.wait_ge(whT_hi_ready, t + 1)
                tt(whT_lo[:, :], p_whT, whT_hi[:, :].bitcast(F32), ALU.subtract).then_inc(whT_ready, 1)

            def finish(t, buffer, halves=(0, 1), product=p_s3):
                for h in halves:
                    dve.wait_ge(s3_done, 2 * t + h + 1)
                    stt(out=x_all[:, bass.ds(t, 1), H * h:H * h + H].rearrange("p a d -> p (a d)"), in0=product[:, h, :], scalar=col(U, t),
                        in1=half(buffer, h), op0=ALU.add, op1=ALU.add).then_inc(res_ready, 1)

            join_main(0, 0, 0)
            join_main(0, 1, 0)
            mean2(0)
            offset(0)
            ln1_stats(3)
            dve.wait_ge(w_sum_done, 1)
            nc.vector.tensor_copy(w_sum[:, :], p_s2[:, 0:W]).then_inc(w_sum_ready, 1)
            join_main(1, 0, 1, p_s3)
            join_main(1, 1, 1, p_s3)
            mean2(1)
            join_main(2, 0, 2)
            dve.wait_ge(w_sum_ready, 1)
            pick(0)
            weigh(0)
            dve.wait_ge(x_in[0], 48)
            half_stats(4, 0)
            split_whT(0)
            link(half_stats(4, 1))
            mean_and_var(4)
            offset(1)
            join_main(2, 1, 2)
            mean2(2)
            finish_clip(4)
            finish_clip(5)
            pick(1)
            weigh(1)
            finish_clip(6)
            finish_clip(7)
            finish(0, 0)

            def period(t, p, finished, more=True):
                if more:
                    half_stats(t + 2, 0)
                split_whT(t - 2)
                if t == 3:
                    finish_clip(8)
                    finish_clip(9)
                if more:
                    link(half_stats(t + 2, 1))
                    mean_and_var(t + 2)
                finish(t - 2, finished)
                dve.wait_ge(res_ready, 2 * t - 2)
                join_main(t, 0, p)
                if t == 3:
                    finish_clip(10)
                    finish_clip(11)
                pick(t - 1)
                join_main(t, 1, p)
                weigh(t - 1)
                mean2(t)
                offset(t - 1)

            dve.wait_ge(x_in[1], 48)
            period(3, 1, 1)
            dve.wait_ge(x_in[0], 64)
            dve.wait_ge(x_in[1], 64)
            period(4, 2, 2)
            period(5, 1, 1)
            period(6, 2, 2, more=False)
            split_whT(5)
            offset(6)
            join_main(7, 0, 0)
            join_main(7, 1, 0)
            mean2(7)
            offset(7)
            pick(6)
            weigh(6)
            finish(5, 1)
            split_whT(6)
            pick(7, p_main[:, 0, :])
            weigh(7)
            finish(6, 2, (0,))
            split_whT(7)
            finish(6, 2, (1,))
            finish(7, 0, product=p_main)

        @block.tensor
        def _(pe):
            def transpose_a1(t, p):
                pe.wait_ge(a1_ready, t + 1)
                pe.wait_ge(a1T_ready, 16 * t)
                for k in range(K):
                    last = nc.tensor.transpose(p_t1[:, P * k:P * k + P], a1[:, p, P * k:P * k + P], ident_b[:, :])
                last.then_inc(t1_done, 1)

            def product(out, b, p, h, k):
                return nc.tensor.matmul(out[:, h, :], a1T[:, p, k, :], q2[:, bass.ds(b * K + k, 1), H * h:H * h + H].rearrange("p a n -> p (a n)"),
                                        start=(k == 0), stop=(k == K - 1))

            def add_rest(out, b, h):
                with nc.tensor.If(has_rest != 0):
                    for k in range(K):
                        for part in range(3):
                            nc.tensor.matmul(out[:, h, :], rest[:, part, :], q2[:, bass.ds(b * K + k, 1), H * h:H * h + H].rearrange("p a n -> p (a n)"),
                                             start=False, stop=False)

            def main(b, p, h, k0, k1):
                for k in range(k0, k1):
                    if k == K - 1:
                        add_rest(p_main, b, h)
                    last = product(p_main, b, p, h, k)
                if k1 == K:
                    last.then_inc(main_done, 1)

            def transpose_x2(t, p):
                for h in range(2):
                    pe.wait_ge(x2_ready, 2 * t + h + 1)
                    for k in range(4 * h, 4 * h + 4):
                        last = nc.tensor.transpose(p_t2[:, h, P * (k % 4):P * (k % 4) + P], x2[:, p, P * k:P * k + P], ident[:, :])
                    last.then_inc(t2_done, 1)

            def logits_and_h(t, p, p_s2=p_s2):
                for k in range(K):
                    if k % 4 == 0:
                        pe.wait_ge(x2T_ready, 2 * t + k // 4 + 1)
                    last = nc.tensor.matmul(p_s2[:, 0:W], x2T[:, p, k, :], wT[:, k, :], start=(k == 0), stop=(k == K - 1))
                last.then_inc(s2_done, 1)

            def transpose_wh(t):
                pe.wait_ge(wh_ready, t + 1)
                nc.tensor.transpose(p_whT, wh[:, :], ident[:, :]).then_inc(t3_done, 1)

            def lora_out(t, out=p_s3):
                pe.wait_ge(whT_ready, t + 1)
                for h in range(2):
                    n = slice(H * h, H * h + H)
                    nc.tensor.matmul(out[:, h, :], whT_hi[:, :], b_hi[:, n], start=True, stop=False)
                    nc.tensor.matmul(out[:, h, :], whT_hi[:, :], b_lo[:, n], start=False, stop=False)
                    nc.tensor.matmul(out[:, h, :], whT_lo[:, :], b_hi[:, n], start=False, stop=True).then_inc(s3_done, 1)

            pe.wait_ge(const_ready, 4)
            transpose_a1(0, 0)
            pe.wait_ge(a1T_ready, 16)
            for k in range(4):
                pe.wait_ge(q2_ready, k + 1)
                for h in range(2):
                    product(p_main, 0, 0, h, k)
                if k == 1:
                    transpose_a1(1, 1)
            pe.wait_ge(a1T_ready, 32)
            for k in range(4):
                for h in range(2):
                    product(p_s3, 0, 1, h, k)
            pe.wait_ge(rest_ready, 1)
            has_rest = pe.value_load(flag[0:1, 0:1], min_val=0, max_val=1)
            for k in range(4, K):
                pe.wait_ge(q2_ready, k + 1)
                for p, out in enumerate((p_main, p_s3)):
                    for h in range(2):
                        if k == K - 1:
                            add_rest(out, 0, h)
                        last = product(out, 0, p, h, k)
                        if k == K - 1:
                            last.then_inc(main_done, 1)
            transpose_a1(2, 0)
            transpose_x2(0, 0)
            pe.wait_ge(w_folded, 1)
            nc.tensor.matmul(p_s2[:, 0:W], ones[:, :], w_fold[:, 6, :], start=True, stop=True).then_inc(w_sum_done, 1)
            pe.wait_ge(a1T_ready, 48)
            main(0, 0, 0, 0, K)
            pe.wait_ge(w_sum_ready, 1)
            logits_and_h(0, 0)
            pe.wait_ge(x2T_ready, 2)
            transpose_x2(1, 1)
            main(0, 0, 1, 0, 4)
            transpose_wh(0)
            main(0, 0, 1, 4, K)
            pe.wait_ge(whT_ready, 1)
            logits_and_h(1, 1)
            transpose_a1(3, 1)
            pe.wait_ge(b_lo_ready, 1)
            lora_out(0)

            def period(t, p, b, x2_buffer, last=False):
                pe.wait_ge(a1T_ready, 16 * (t + 1))
                pe.wait_ge(x2_ready, 2 * t - 1)
                main(b, p, 0, 0, K - 2)
                if p == 0:
                    pe.wait_ge(q2_ready, 2 * K)
                main(b, p, 0, K - 2, K)
                pe.wait_ge(x2T_ready, 2 * t - 2)
                transpose_x2(t - 1, x2_buffer)
                transpose_wh(t - 2)
                main(b, p, 1, 0, 4)
                if last:
                    main(b, p, 1, 4, K)
                    pe.wait_ge(whT_ready, t - 1)
                    logits_and_h(t - 1, 1 - p)
                    pe.wait_ge(x2T_ready, 2 * t)
                    transpose_x2(t, 0)
                pe.wait_ge(res_ready, 2 * t - 4)
                lora_out(t - 2)
                if not last:
                    logits_and_h(t - 1, 1 - p)
                    main(b, p, 1, 4, K)

            with pe.Fori(0, 2) as i:
                period(2 * i + 3, 1, i, 2)
                pe.wait_ge(q2_ready, 2 * K - 2)
                period(2 * i + 4, 0, 1, 1)
            period(7, 1, 1, 2, last=True)
            transpose_wh(6)
            logits_and_h(7, 1, p_main[:, 0, :])
            pe.wait_ge(res_ready, 12)
            lora_out(6)
            transpose_wh(7)
            lora_out(7, p_main)


def kernel(**inputs):
    import numpy as _np
    import concourse.bacc as _bacc
    from concourse import mybir as _mybir
    from concourse.bass_utils import run_bass_kernel_spmd as _run

    a = {k: _np.asarray(v) for k, v in inputs.items()}
    experts, rank, d = a["L0_ffn_A"].shape
    k = d // 128
    w = _np.concatenate([a["L0_ffn_route_w"].T, a["L0_ffn_A"].reshape(experts * rank, d).T], axis=1)
    arrays = {
        "x": a["x"],
        "ctx": a["ctx_4096"],
        "given": _np.concatenate([a["L0_xattn_x1_scale"], a["L0_xattn_x1_zp"], a["L0_xattn_x2_scale"], a["L0_xattn_x2_zp"]]),
        "down": w.reshape(k, 128, w.shape[1]).transpose(1, 0, 2).reshape(128, k * w.shape[1]),
        "up": a["L0_ffn_Bw"].transpose(0, 2, 1).reshape(experts * rank, -1),
    }
    arrays = {f"in_{n}_dram": _np.ascontiguousarray(v) for n, v in arrays.items()}
    nc = _bacc.Bacc("TRN2", target_bir_lowering=False, num_devices=1)
    args = [nc.dram_tensor(n, v.shape, _mybir.dt.from_np(v.dtype), kind="ExternalInput").ap() for n, v in arrays.items()]
    args.append(nc.dram_tensor("out_0_dram", (2, 512, 1024), _mybir.dt.from_np(_np.dtype("float32")), kind="ExternalOutput").ap())
    build(nc, *args)
    return _run(nc, [arrays], core_ids=[0]).results[0]["out_0_dram"]
```
